# Optimizing a Trainium2 kernel written in Bass

```python
import numpy as np
import jax
import jax.numpy as jnp

def _softmax(x, axis=-1):
    return jax.nn.softmax(x, axis=axis)

def _gelu(x):
    return jax.nn.gelu(x, approximate=True)

def _silu(x):
    return jax.nn.silu(x)

def _sigmoid(x):
    return jax.nn.sigmoid(x)

def _layernorm(x, axis=-1, eps=1e-05):
    m = jnp.mean(x, axis=axis, keepdims=True)
    v = jnp.var(x, axis=axis, keepdims=True)
    return (x - m) / jnp.sqrt(v + eps)

def _scatter_add(tgt, idx, src, axis=0):
    return tgt.at[idx].add(src)

def _segment_sum(src, seg, n):
    return jax.ops.segment_sum(src, seg, n)
kernel_name = 'mk_decoder_preln_d1_seqx_r8_940389'

def setup_inputs(seed: int=0):
    np.random.seed(seed)
    _w = jnp.asarray

    def _rec_inputs():
        import jax
        import jax.numpy as jnp
        _rk = jax.random.key(seed)
        x = -7.109e-05 + 0.9999 * jax.random.normal(jax.random.fold_in(_rk, 1), (4, 256, 256), jnp.float32)
        _lenS = 256 - jax.random.randint(jax.random.fold_in(_rk, 7), (4,), 0, max(1, 256 // 4) + 1, jnp.int32)
        _lenS2 = 256 - jax.random.randint(jax.random.fold_in(_rk, 8), (4,), 0, max(1, 256 // 4) + 1, jnp.int32)
        _ctx_512P = jax.random.normal(jax.random.fold_in(_rk, 11), (4, 16, 64), jnp.float32)
        _ctx_512c = jax.random.dirichlet(jax.random.fold_in(_rk, 511), 0.3 * jnp.ones((16,), jnp.float32), (4, 256))
        _ctx_512t = jnp.einsum('bsk,bkd->bsd', _ctx_512c, _ctx_512P)
        _ctx_512t = _ctx_512t * jax.lax.rsqrt(jnp.mean(jnp.square(_ctx_512t)) + 1e-12) * 0.953939
        ctx_512 = 2.81802e-05 + 1.00001 * (_ctx_512t + 0.3 * jax.random.normal(jax.random.fold_in(_rk, 611), (4, 256, 64), jnp.float32))
        return (x, ctx_512)
    x, ctx_512 = _rec_inputs()

    def _L0_attn_setup():
        import jax, jax.numpy as jnp
        import numpy as np
        DECAY = 0.95

        def smear(x, decay):
            a = jnp.full_like(x, decay)

            def combine(c1, c2):
                a1, b1 = c1
                a2, b2 = c2
                return (a1 * a2, a2 * b1 + b2)
            _, y = jax.lax.associative_scan(combine, (a, x), axis=1)
            return y
        key = jax.random.key(seed)
        ks = jax.random.split(key, 5)
        B, S, E, M = (4, 512, 256, 256)
        x = jax.random.normal(ks[0], (B, S, E), dtype=jnp.float32)
        s = 0.02
        Wv = jax.random.normal(ks[1], (E, M), dtype=jnp.float32) * s
        Wg = jax.random.normal(ks[2], (E, M), dtype=jnp.float32) * s
        bg = jnp.zeros((M,), dtype=jnp.float32)
        Wq = jax.random.normal(ks[3], (E, M), dtype=jnp.float32) * s
        bq = jnp.zeros((M,), dtype=jnp.float32)
        Wo = jax.random.normal(ks[4], (M, E), dtype=jnp.float32) * s
        return {'x': x, 'Wv': Wv, 'Wg': Wg, 'bg': bg, 'Wq': Wq, 'bq': bq, 'Wo': Wo}
    _L0_attn_all = _L0_attn_setup()
    _L0_attn_in = {k: v for k, v in _L0_attn_all.items() if k in ('Wv', 'Wg', 'bg', 'Wq', 'bq', 'Wo')}
    del _L0_attn_all

    def _L0_xattn_setup():
        import jax, jax.numpy as jnp
        import numpy as np
        EPS = 1e-06
        IMAGE_DIMS = 256
        key = jax.random.key(seed)
        k1, k2, k3 = jax.random.split(key, 3)
        B, I, J, D = (16, 256, 256, 64)
        p = jax.random.normal(k1, (B, I, J), dtype=jnp.float32)
        k_v = jax.random.normal(k2, (B, J, D), dtype=jnp.float32)
        W_k = jax.random.normal(k3, (D, D), dtype=jnp.float32) * (1.0 / np.sqrt(D))
        b_k = jnp.zeros((D,), dtype=jnp.float32)
        ln_gamma = jnp.ones((J,), dtype=jnp.float32)
        ln_beta = jnp.zeros((J,), dtype=jnp.float32)
        return {'p': p, 'k_v': k_v, 'W_k': W_k, 'b_k': b_k, 'ln_gamma': ln_gamma, 'ln_beta': ln_beta}
    _L0_xattn_all = _L0_xattn_setup()
    _L0_xattn_in = {k: v for k, v in _L0_xattn_all.items() if k in ('W_k', 'b_k', 'ln_gamma', 'ln_beta')}
    del _L0_xattn_all

    def _L0_ffn_setup():
        import jax, jax.numpy as jnp
        import numpy as np
        SEQ, BS, D, F, E = (128, 2, 256, 256, 8)
        key = jax.random.key(seed)
        ks = jax.random.split(key, 8)
        s = 0.02
        return {'hidden_states': jax.random.normal(ks[0], (SEQ, BS, D), jnp.float32), 'router_w': jax.random.normal(ks[1], (D, E), jnp.float32) * s, 'gate_w': jax.random.normal(ks[2], (E, D, F), jnp.float32) * s, 'up_w': jax.random.normal(ks[3], (E, D, F), jnp.float32) * s, 'down_w': jax.random.normal(ks[4], (E, F, D), jnp.float32) * s, 'shared_gate_w': jax.random.normal(ks[5], (D, F), jnp.float32) * s, 'shared_up_w': jax.random.normal(ks[6], (D, F), jnp.float32) * s, 'shared_down_w': jax.random.normal(ks[7], (F, D), jnp.float32) * s}
    _L0_ffn_all = _L0_ffn_setup()
    _L0_ffn_in = {k: v for k, v in _L0_ffn_all.items() if k in ('router_w', 'gate_w', 'up_w', 'down_w', 'shared_gate_w', 'shared_up_w', 'shared_down_w')}
    del _L0_ffn_all
    return {'x': x, 'ctx_512': ctx_512, 'L0_attn_Wv': _L0_attn_in['Wv'], 'L0_attn_Wg': _L0_attn_in['Wg'], 'L0_attn_bg': _L0_attn_in['bg'], 'L0_attn_Wq': _L0_attn_in['Wq'], 'L0_attn_bq': _L0_attn_in['bq'], 'L0_attn_Wo': _L0_attn_in['Wo'], 'L0_xattn_W_k': _L0_xattn_in['W_k'], 'L0_xattn_b_k': _L0_xattn_in['b_k'], 'L0_xattn_ln_gamma': _L0_xattn_in['ln_gamma'], 'L0_xattn_ln_beta': _L0_xattn_in['ln_beta'], 'L0_ffn_router_w': _L0_ffn_in['router_w'], 'L0_ffn_gate_w': _L0_ffn_in['gate_w'], 'L0_ffn_up_w': _L0_ffn_in['up_w'], 'L0_ffn_down_w': _L0_ffn_in['down_w'], 'L0_ffn_shared_gate_w': _L0_ffn_in['shared_gate_w'], 'L0_ffn_shared_up_w': _L0_ffn_in['shared_up_w'], 'L0_ffn_shared_down_w': _L0_ffn_in['shared_down_w']}

def reference(x, ctx_512, L0_attn_Wv, L0_attn_Wg, L0_attn_bg, L0_attn_Wq, L0_attn_bq, L0_attn_Wo, L0_xattn_W_k, L0_xattn_b_k, L0_xattn_ln_gamma, L0_xattn_ln_beta, L0_ffn_router_w, L0_ffn_gate_w, L0_ffn_up_w, L0_ffn_down_w, L0_ffn_shared_gate_w, L0_ffn_shared_up_w, L0_ffn_shared_down_w):
    import jax
    import jax.numpy as jnp

    def _L0_attn_ref(x, Wv, Wg, bg, Wq, bq, Wo):
        import jax, jax.numpy as jnp
        import numpy as np
        DECAY = 0.95

        def smear(x, decay):
            a = jnp.full_like(x, decay)

            def combine(c1, c2):
                a1, b1 = c1
                a2, b2 = c2
                return (a1 * a2, a2 * b1 + b2)
            _, y = jax.lax.associative_scan(combine, (a, x), axis=1)
            return y
        scale = jnp.float32(np.sqrt(1.0 - DECAY))
        gate = jax.nn.sigmoid(jnp.einsum('bse,em->bsm', x, Wg) + bg)
        store = jnp.einsum('bse,em->bsm', x, Wv) * gate * scale
        mem = smear(store, DECAY)
        que = jax.nn.sigmoid(jnp.einsum('bse,em->bsm', x, Wq) + bq)
        load = mem * que * scale
        return jnp.einsum('bsm,me->bse', load, Wo)

    def _L0_xattn_ref(p, k_v, W_k, b_k, ln_gamma, ln_beta):
        import jax, jax.numpy as jnp
        import numpy as np
        EPS = 1e-06
        IMAGE_DIMS = 256
        kv = k_v @ W_k.T + b_k
        out = jnp.einsum('bij,bjd->bid', p, kv)
        scale = IMAGE_DIMS ** (-0.5)
        sim = jnp.einsum('bid,bjd->bij', out, kv) * scale
        mu = jnp.mean(sim, axis=-1, keepdims=True)
        var = jnp.var(sim, axis=-1, keepdims=True)
        sim = (sim - mu) * jax.lax.rsqrt(var + EPS) * ln_gamma + ln_beta
        attn = jax.nn.softmax(sim, axis=-1)
        return attn

    def _L0_ffn_ref(hidden_states, router_w, gate_w, up_w, down_w, shared_gate_w, shared_up_w, shared_down_w):
        import jax, jax.numpy as jnp
        import numpy as np
        SEQ, BS, D, F, E = (128, 2, 256, 256, 8)
        S, B, Dm = hidden_states.shape
        x = hidden_states.reshape(-1, Dm)
        logits = x @ router_w
        expert_idx = jnp.argmax(logits, axis=-1)
        score = jax.nn.sigmoid(jnp.max(logits, axis=-1))
        xs = x * score[:, None]
        n_experts = router_w.shape[1]
        out = jnp.zeros_like(x)
        for e in range(n_experts):
            m = (expert_idx == e)[:, None]
            xe = jnp.where(m, xs, 0.0)
            h = jax.nn.silu(xe @ gate_w[e]) * (xe @ up_w[e])
            out = out + jnp.where(m, h @ down_w[e], 0.0)
        shared = jax.nn.silu(x @ shared_gate_w) * (x @ shared_up_w) @ shared_down_w
        return (out + shared).reshape(S, B, Dm)
    x = x + _L0_attn_ref(_layernorm(x, axis=-1), L0_attn_Wv, L0_attn_Wg, L0_attn_bg, L0_attn_Wq, L0_attn_bq, L0_attn_Wo)
    x = x + _L0_xattn_ref(_layernorm(x, axis=-1), ctx_512, L0_xattn_W_k, L0_xattn_b_k, L0_xattn_ln_gamma, L0_xattn_ln_beta)
    x = x + _L0_ffn_ref(_layernorm(x, axis=-1), L0_ffn_router_w, L0_ffn_gate_w, L0_ffn_up_w, L0_ffn_down_w, L0_ffn_shared_gate_w, L0_ffn_shared_up_w, L0_ffn_shared_down_w)
    return x

_drawn_inputs = setup_inputs


def setup_inputs(seed=0):
    import zlib

    import numpy as np

    out = dict(_drawn_inputs(seed))
    spreads = {'L0_attn_bg': (0.0, 0.8),
     'L0_attn_bq': (0.0, 0.8),
     'L0_xattn_b_k': (0.0, 0.8),
     'L0_xattn_ln_gamma': (1.0, 0.6),
     'L0_xattn_ln_beta': (0.0, 0.8)}
    factors = {'ctx_512': 8.0,
     'L0_attn_Wv': 8.0,
     'L0_attn_Wg': 8.0,
     'L0_attn_Wq': 8.0,
     'L0_attn_Wo': 8.0,
     'L0_xattn_W_k': 8.0,
     'L0_ffn_router_w': 8.0,
     'L0_ffn_gate_w': 8.0,
     'L0_ffn_up_w': 8.0,
     'L0_ffn_down_w': 8.0,
     'L0_ffn_shared_gate_w': 3.381,
     'L0_ffn_shared_up_w': 3.336,
     'L0_ffn_shared_down_w': 3.337}
    for name, (base, spread) in spreads.items():
        noise = np.random.default_rng([zlib.crc32(name.encode()), seed]).standard_normal(out[name].shape)
        drawn = base * np.exp(spread * noise) if base else spread * noise
        out[name] = jnp.asarray(drawn.astype(out[name].dtype))
    for name, factor in factors.items():
        out[name] = (out[name] * factor).astype(out[name].dtype)
    return out
```

```python
from contextlib import ExitStack

import concourse.bass as bass
from concourse import mybir
from concourse.alu_op_type import AluOpType as ALU

ACT = mybir.ActivationFunctionType
AX = mybir.AxisListType
F32 = mybir.dt.float32
F32R = mybir.dt.float32r
BF16 = mybir.dt.bfloat16
U32 = mybir.dt.uint32
I32 = mybir.dt.int32

P = 128
LN_EPS = 1e-5
SIM_EPS = 1e-6
DECAY = 0.95


def decoder_kernel(nc, x, ctx_in, Wv, Wg, bg, Wq, bq, Wo, W_k, b_k, gamma, beta,
                   router_w, gate_w, up_w, down_w, sh_gate_w, sh_up_w, sh_down_w, out):
    B, S, D = x.shape
    C = ctx_in.shape[2]
    E = router_w.shape[1]
    KT = D // P
    TB = S // P
    NT = B * TB
    NS = (B * S + E * (P - 1)) // P
    SIM_SCALE = float(D) ** -0.5
    MEM_SCALE = 0.25 * (1.0 - DECAY)
    ROUTED_PEEL = 3
    ROUTED_LOOPS = (NS - 2 - ROUTED_PEEL) // 2
    SMALL = 4 + 2 * KT
    RING = 4

    x_sorted = nc.dram_tensor("x_sorted", (NS * P, D), F32, kind="Internal").ap()
    y_sorted = nc.dram_tensor("y_sorted", (NS * P, D), F32, kind="Internal").ap()

    with ExitStack() as ctx:
        def sb(name, shape, dt=F32):
            return ctx.enter_context(nc.sbuf_tensor(name, shape, dt))

        def bank(name):
            return ctx.enter_context(nc.psum_tensor(name, [P, 512], F32))

        def sem(name):
            return ctx.enter_context(nc.semaphore(name))

        res = sb("res", [P, NT, D])
        xs = sb("xs", [P, NT, D])
        ctxT = xs[0:C, 0:NT // 2, :].rearrange("p t n -> p (t n)")
        kvT = xs[0:C, NT // 2:NT, :].rearrange("p t n -> p (t n)")
        xn1 = sb("xn1", [P, 2, TB, D])
        xn2 = sb("xn2", [P, TB, D])
        xn3 = sb("xn3", [P, TB, D])
        xT1_hi = sb("xT1_hi", [P, 2, KT, S], F32R)
        xT1_lo = sb("xT1_lo", [P, 2, KT, S], F32R)
        xT2_hi = sb("xT2_hi", [P, KT, S], F32R)
        xT2_lo = sb("xT2_lo", [P, KT, S], F32R)
        xT3_hi = sb("xT3_hi", [P, KT, S], F32R)
        xT3_lo = sb("xT3_lo", [P, KT, S], F32R)
        gqvo_hi = sb("gqvo_hi", [P, 4, KT, D], F32R)
        gqvo_lo = sb("gqvo_lo", [P, 4, KT, D], F32R)
        shw_hi = sb("shw_hi", [P, 3, KT, D], F32R)
        shw_lo = sb("shw_lo", [P, 3, KT, D], F32R)
        gu_hi = sb("gu_hi", [P, E, KT, 2 * D], F32R)
        gu_lo = sb("gu_lo", [P, E, KT, 2 * D], F32R)
        dn_hi = sb("dn_hi", [P, E, KT, D], F32R)
        dn_lo = sb("dn_lo", [P, E, KT, D], F32R)
        gram_hi = gu_hi[:, E - 2:E, :, :].rearrange("p e k n -> p (e k n)").rearrange(
            "p (b k n) -> p b k n", b=B, k=KT)
        gram_lo = gu_lo[:, E - 2:E, :, :].rearrange("p e k n -> p (e k n)").rearrange(
            "p (b k n) -> p b k n", b=B, k=KT)
        stage = sb("stage", [P, RING, KT, D])
        tg = sb("tg", [P, KT, S])
        tq = sb("tq", [P, KT, S])
        mem = sb("mem", [P, KT, S])
        ld_hi = sb("ld_hi", [P, KT, S], F32R)
        ld_lo = sb("ld_lo", [P, KT, S], F32R)
        z = sb("z", [P, TB, S])
        ez = sb("ez", [P, TB, S])
        hs = sb("hs", [P, KT, S])
        hs_hi = sb("hs_hi", [P, KT, S], F32R)
        hs_lo = sb("hs_lo", [P, KT, S], F32R)
        ctx_nat = sb("ctx_nat", [P, NT, C])
        wk_nat = sb("wk_nat", [C, C])
        wkT = sb("wkT", [C, C])
        bk = sb("bk", [C, 1])
        hb = sb("hb", [P, 2, KT])
        gam = sb("gam", [P, S])
        bet = sb("bet", [P, S])
        decay = sb("decay", [P, S])
        zero = sb("zero", [P, D])
        ident = sb("ident", [P, P])
        below = sb("below", [P, P], BF16)
        ones = sb("ones", [P, P], BF16)
        expo = sb("expo", [P, TB])
        rw = sb("rw", [P, KT, E])
        rw_hi = sb("rw_hi", [P, KT, E], F32R)
        rw_lo = sb("rw_lo", [P, KT, E], F32R)
        io_e = sb("io_e", [P, TB, E])
        io_e8 = sb("io_e8", [P, TB, E])
        io_k = sb("io_k", [P, E, NT])
        io_s = sb("io_s", [1, NS, E])
        bn = sb("bn", [P, 4, TB, 6])
        mv = sb("mv", [P, 4, TB, 2])
        vareps = sb("vareps", [P, 4, TB])
        rstd = sb("rstd", [P, 4, TB])
        nmr = sb("nmr", [P, TB])
        nmax = sb("nmax", [P, TB])
        ssum = sb("ssum", [P, TB])
        rsum = sb("rsum", [P, TB])
        lg = sb("lg", [P, TB, E])
        mx = sb("mx", [P, TB])
        sct = sb("sct", [P, TB])
        score = sb("score", [P, TB])
        cand = sb("cand", [P, TB, E])
        idx = sb("idx", [P, TB])
        onehot = sb("onehot", [P, NT + 1, E], BF16)
        cmp_k = sb("cmp_k", [P, E, NT])
        ntile = sb("ntile", [P, E])
        one_e = sb("one_e", [P, E])
        incl = sb("incl", [P, E])
        excl = sb("excl", [P, E])
        slot_a = sb("slot_a", [P, NT, E])
        slot_b = sb("slot_b", [P, NT, E])
        dest_f = sb("dest_f", [P, NT])
        dest = sb("dest", [P, NT], U32)
        cmp_s = sb("cmp_s", [1, NS, E])
        te_f = sb("te_f", [1, NS])
        te = sb("te", [1, NS], I32)
        xg = mem
        xgT_hi, xgT_lo = xT1_hi[:, :, :, 0:P], xT1_lo[:, :, :, 0:P]
        hT_hi, hT_lo = xT1_hi[:, :, :, P:2 * P], xT1_lo[:, :, :, P:2 * P]
        rh = tg
        ry = tq

        bT, bU, bG, bQ, bV, bO, bS, bM = [bank(n) for n in ("bT", "bU", "bG", "bQ", "bV", "bO", "bS", "bM")]

        def halves(b):
            return b[:, :].rearrange("p (k n) -> p k n", k=2)

        psT, psU, psG, psQ, psV, psO, psS, psM = [halves(b) for b in (bT, bU, bG, bQ, bV, bO, bS, bM)]
        ps_lg = bM[:, 0:TB * E].rearrange("p (t e) -> p t e", e=E)
        ps_rank = bM[:, 128:128 + (NT + 1) * E].rearrange("p (t e) -> p t e", e=E)
        rank = ps_rank[:, 0:NT, :]
        count = ps_rank[:, NT, :]

        def transposed_tile(b):
            return b[:, 0:KT * P].rearrange("p (k n) -> p k n", k=KT)

        psX, psH = [transposed_tile(bT), transposed_tile(bS)], [transposed_tile(bU), transposed_tile(bM)]
        psGU, psY = [bG, bQ], [psV, psO]

        x_in = [sem(f"x_in{b}") for b in range(B)]
        ctx_loaded, small_loaded, rw_loaded = sem("ctx_loaded"), sem("small_loaded"), sem("rw_loaded")
        rw_split = sem("rw_split")
        stage_in = [sem(f"stage_in{r}") for r in range(RING)]
        unit_hi, unit_lo = sem("unit_hi"), sem("unit_lo")
        ident_raw, ident_made, consts_made, dve_consts = sem("ident_raw"), sem("ident_made"), sem("consts_made"), sem("dve_consts")
        below_raw = sem("below_raw")
        half_bias = sem("half_bias")
        stats, bn_raw, eps_added, rstd_made = sem("stats"), sem("bn_raw"), sem("eps_added"), sem("rstd_made")
        names = ("xn1_made", "t1_done", "xT1_hi_made", "xT1_lo_made", "g_done", "q_done", "v_done",
                 "tg_made", "tq_made", "stored", "scanned", "loaded", "ld_hi_made", "ld_lo_made", "o_done",
                 "x2_made", "xn2_made", "t2_done", "xT2_hi_made", "xT2_lo_made", "sim_done", "nmr_made",
                 "zn_made", "zg_made", "z_made", "max_made", "exp_made", "rsum_made", "x3_made", "xn3_made",
                 "t3_done", "xT3_hi_made", "xT3_lo_made", "lg_done", "lg_copied", "mx_made", "sct_made",
                 "score_made", "xs_made", "eq_made", "cand_made", "idx_made", "onehot_made",
                 "shg_done", "shu_done", "th_made", "ht_made", "h_made", "hs_hi_made", "hs_lo_made",
                 "sd_done", "base_made")
        sm = {n: sem(n) for n in names}
        wk_t, wkT_made, ctx_t, ctxT_made, kv_done, kvT_made = (
            sem("wk_t"), sem("wkT_made"), sem("ctx_t"), sem("ctxT_made"), sem("kv_done"), sem("kvT_made"))
        gram_done, gram_hi_made, gram_lo_made = sem("gram_done"), sem("gram_hi_made"), sem("gram_lo_made")
        rank_done, route_step, dest_made, te_made = sem("rank_done"), sem("route_step"), sem("dest_made"), sem("te_made")
        zeroed, scattered = sem("zeroed"), sem("scattered")
        xg_in = [sem("xg_in0"), sem("xg_in1")]
        tx_done, xg_hi_made, xg_lo_made = sem("tx_done"), sem("xg_hi_made"), sem("xg_lo_made")
        gu_done, rth_made, rt_made, rh_made = sem("gu_done"), sem("rth_made"), sem("rt_made"), sem("rh_made")
        th_done, hT_hi_made, hT_lo_made = sem("th_done"), sem("hT_hi_made"), sem("hT_lo_made")
        down_done, y_made = sem("down_done"), sem("y_made")
        y_out = [sem("y_out0"), sem("y_out1")]
        gathered = [sem(f"gathered{t}") for t in range(NT)]
        final_made, written = sem("final_made"), sem("written")

        def rows(w):
            return w.rearrange("(k p) n -> p k n", p=P)

        units = [(rows(w), gqvo_hi[:, i], gqvo_lo[:, i]) for i, w in enumerate((Wg, Wq, Wv, Wo))]
        units += [(rows(w), shw_hi[:, i], shw_lo[:, i]) for i, w in enumerate((sh_gate_w, sh_up_w, sh_down_w))]
        for e in range(E):
            units += [(rows(gate_w[e]), gu_hi[:, e, :, 0:D], gu_lo[:, e, :, 0:D]),
                      (rows(up_w[e]), gu_hi[:, e, :, D:2 * D], gu_lo[:, e, :, D:2 * D]),
                      (rows(down_w[e]), dn_hi[:, e], dn_lo[:, e])]
        U_G, U_Q, U_V, U_O, U_SG, U_SU, U_SD = range(7)
        PLAN = [(3, 4), (4, 8), (8, 12), (12, 16), (16, 20), (20, 25), (25, len(units))]
        GRAM_UNIT = 7 + 3 * (E - 2)
        STEPS = B + 3
        LN1, LN2, SIM, LN3 = range(4)
        NORMS = [(LN1, 0)]
        for k in range(STEPS):
            NORMS += [(kind, b) for kind, b in ((LN1, k + 1), (LN2, k - 1), (SIM, k - 2), (LN3, k - 2)) if 0 <= b < B]

        def nth(kind, b):
            return NORMS.index((kind, b)) + 1

        def f32(ap):
            return ap.bitcast(F32)

        block = ctx.enter_context(nc.Block())

        @block.sync
        def _(sp):
            def load_x(b):
                sp.dma_start(res[:, b * TB:(b + 1) * TB, :], x[b].rearrange("(t p) d -> p t d", p=P)).then_inc(x_in[b], 16)

            def load_unit(n):
                if n >= RING:
                    sp.wait_ge(unit_hi, n - RING + 1)
                    sp.wait_ge(unit_lo, n - RING + 1)
                sp.dma_start(stage[:, n % RING], units[n][0]).then_inc(stage_in[n % RING], 16)

            load_x(0)
            load_unit(U_G)
            load_unit(U_Q)
            load_unit(U_V)
            sp.dma_start(ctx_nat[:, :, :], ctx_in.rearrange("b (t p) c -> p (b t) c", p=P)).then_inc(ctx_loaded, 16)
            load_x(1)
            load_unit(U_O)
            load_x(2)
            load_x(3)
            for n in range(RING, len(units)):
                load_unit(n)
                if n == 14:
                    sp.wait_ge(dve_consts, 1)
                    sp.dma_start(x_sorted.rearrange("(s p) d -> p s d", p=P),
                                 zero[:, :].unsqueeze(1).to_broadcast([P, NS, D])).then_inc(zeroed, 16)

            sp.wait_ge(scattered, 16 * NT)

            def load_rows(s, r):
                sp.dma_start(xg[:, r, :], x_sorted[bass.ds(s * P, P), :]).then_inc(xg_in[r], 16)

            load_rows(0, 0)
            load_rows(1, 1)
            with sp.Fori(0, (NS - 3) // 2) as i:
                for r in range(2):
                    sp.wait_ge(tx_done, i * 2 + (r + 1))
                    load_rows(i * 2 + (r + 2), r)
            sp.wait_ge(tx_done, NS - 2)
            load_rows(NS - 1, (NS - 1) % 2)
            for b in range(B):
                sp.wait_ge(final_made, b + 1)
                sp.dma_start(out[b].rearrange("(t p) d -> p t d", p=P), res[:, b * TB:(b + 1) * TB, :]).then_inc(written, 16)
            sp.wait_ge(written, 16 * B)

        @block.gpsimd
        def _(pool):
            g = nc.gpsimd
            g.memset(ident[:, :], 0.0).then_inc(ident_raw, 1)
            g.memset(expo[:, :], -0.5).then_inc(ident_raw, 1)
            pool.wait_ge(ident_raw, 2)
            g.affine_select(out=ident[:, :], in_=ident[:, :], compare_op=ALU.not_equal, fill=1.0, base=0,
                            pattern=[[-1, P]], channel_multiplier=1).then_inc(ident_made, 1)

            def rsqrt(kind, b):
                n = nth(kind, b)
                eps = SIM_EPS / SIM_SCALE ** 2 if kind == SIM else LN_EPS
                pool.wait_ge(stats, n)
                g.tensor_scalar(vareps[:, kind, :], mv[:, kind, :, 1], eps, None, ALU.add).then_inc(eps_added, 1)
                pool.wait_ge(eps_added, n)
                g.tensor_tensor(rstd[:, kind, :], vareps[:, kind, :], expo[:, :], ALU.pow).then_inc(rstd_made, 1)

            def unit(n):
                pool.wait_ge(unit_hi, n + 1)
                g.tensor_tensor(units[n][2], stage[:, n % RING], f32(units[n][1]), ALU.subtract).then_inc(unit_lo, 1)

            def consts():
                g.memset(below[:, :], 1.0).then_inc(below_raw, 1)
                g.iota(io_e[:, :, :], [[0, TB], [1, E]], 0, 0, True)
                g.iota(io_e8[:, :, :], [[0, TB], [1, E]], -E, 0, True)
                g.iota(io_k[:, :, :], [[0, E], [P, NT]], 0, 0, True)
                g.iota(io_s[:, :, :], [[1, NS], [0, E]], 0, 0, True)
                pool.wait_ge(below_raw, 1)
                g.affine_select(out=below[:, :], in_=below[:, :], compare_op=ALU.is_gt, fill=0.0, base=0,
                                pattern=[[1, P]], channel_multiplier=-1).then_inc(consts_made, 1)

            rsqrt(LN1, 0)
            for n in range(3):
                unit(n)
            for k in range(STEPS):
                if k + 1 < B:
                    rsqrt(LN1, k + 1)
                if k < B:
                    pool.wait_ge(sm["ld_hi_made"], k + 1)
                    g.tensor_tensor(ld_lo[:, :, :], tq[:, :, :], f32(ld_hi[:, :, :]), ALU.subtract).then_inc(sm["ld_lo_made"], 1)
                if 0 <= k - 1 < B:
                    rsqrt(LN2, k - 1)
                if 0 <= k - 2 < B:
                    rsqrt(SIM, k - 2)
                    pool.wait_ge(sm["zn_made"], k - 1)
                    if k == 2:
                        pool.wait_ge(small_loaded, 16 * SMALL)
                    g.tensor_tensor(z[:, :, :], z[:, :, :], gam[:, :].unsqueeze(1).to_broadcast([P, TB, S]), ALU.mult).then_inc(sm["zg_made"], 1)
                    pool.wait_ge(sm["zg_made"], k - 1)
                    g.tensor_tensor(z[:, :, :], z[:, :, :], bet[:, :].unsqueeze(1).to_broadcast([P, TB, S]), ALU.add).then_inc(sm["z_made"], 1)
                if 0 <= k - 3 < B:
                    pool.wait_ge(sm["hs_hi_made"], k - 2)
                    g.tensor_tensor(hs_lo[:, :, :], hs[:, :, :], f32(hs_hi[:, :, :]), ALU.subtract).then_inc(sm["hs_lo_made"], 1)
                if 0 <= k - 2 < B:
                    rsqrt(LN3, k - 2)
                for n in range(*PLAN[k]):
                    unit(n)
                if k == 0:
                    consts()
            pool.wait_ge(dest_made, 1)
            pool.wait_ge(sm["xs_made"], B)
            pool.wait_ge(zeroed, 16)
            for t in range(NT):
                g.indirect_dma_start(x_sorted, bass.IndirectOffsetOnAxis(dest[:, t:t + 1], 0), xs[:, t, :], None,
                                     bounds_check=NS * P - 1, oob_is_err=False).then_inc(scattered, 16)
            def store_rows(s, r):
                pool.wait_ge(y_made, s + 1)
                pool.dma_start(y_sorted[bass.ds(s * P, P), :], ry[:, r, :]).then_inc(y_out[r], 16)

            with pool.Fori(0, NS // 2) as i:
                for r in range(2):
                    store_rows(i * 2 + r, r)
            store_rows(NS - 1, (NS - 1) % 2)
            pool.wait_ge(scattered, 16 * NT)
            pool.wait_ge(y_out[0], 16 * ((NS + 1) // 2))
            pool.wait_ge(y_out[1], 16 * (NS // 2))
            for t in range(NT):
                g.indirect_dma_start(xs[:, t, :], None, y_sorted, bass.IndirectOffsetOnAxis(dest[:, t:t + 1], 0),
                                     bounds_check=NS * P - 1, oob_is_err=False).then_inc(gathered[t], 16)

        @block.scalar
        def _(act):
            a = nc.scalar

            def load_small():
                act.dma_start(wk_nat[:, :], W_k).then_inc(small_loaded, 16)
                act.dma_start(bk[:, :], b_k.rearrange("(p o) -> p o", o=1)).then_inc(small_loaded, 16)
                for i, bias in enumerate((bg, bq)):
                    for m in range(KT):
                        act.dma_start(hb[:, i, m:m + 1], bias[m * P:(m + 1) * P].rearrange("(p o) -> p o", o=1)).then_inc(small_loaded, 16)
                act.dma_start(gam[:, :], gamma.unsqueeze(0).to_broadcast([P, S])).then_inc(small_loaded, 16)
                act.dma_start(bet[:, :], beta.unsqueeze(0).to_broadcast([P, S])).then_inc(small_loaded, 16)
                act.dma_start(rw[:, :, :], router_w.rearrange("(k p) e -> p k e", p=P)).then_inc(rw_loaded, 16)

            def unit(n):
                act.wait_ge(stage_in[n % RING], 16 * (n // RING + 1))
                if n == GRAM_UNIT:
                    act.wait_ge(sm["sim_done"], B)
                a.copy(units[n][1], stage[:, n % RING]).then_inc(unit_hi, 1)

            def evacuate_hi(src, dst, ready, count, made):
                act.wait_ge(sm[ready], count)
                a.copy(dst, src).then_inc(sm[made], 1)

            load_small()
            for n in range(3):
                unit(n)
            act.wait_ge(small_loaded, 16 * SMALL)
            a.mul(hb[:, :, :], hb[:, :, :], 0.5).then_inc(half_bias, 1)
            act.wait_ge(wk_t, 1)
            a.copy(wkT[:, :], bS[0:C, 0:C]).then_inc(wkT_made, 1)
            for k in range(STEPS):
                if k < B:
                    if k >= 2:
                        act.wait_ge(sm["v_done"], k - 1)
                    evacuate_hi(psT, xT1_hi[:, k % 2], "t1_done", k + 1, "xT1_hi_made")
                    if k == 0:
                        for i, b in enumerate((bO, bQ)):
                            act.wait_ge(ctx_t, i + 1)
                            a.copy(ctxT[:, i * 512:(i + 1) * 512], b[0:C, :]).then_inc(ctxT_made, 1)
                        for i, b in enumerate((bS, bM)):
                            act.wait_ge(kv_done, i + 1)
                            a.activation(kvT[:, i * 512:(i + 1) * 512], b[0:C, :], ACT.Identity, bias=bk[:, :]).then_inc(kvT_made, 1)
                        act.wait_ge(half_bias, 1)
                    for i, (dst, src, ready, made) in enumerate(((tg, psG, "g_done", "tg_made"), (tq, psQ, "q_done", "tq_made"))):
                        act.wait_ge(sm[ready], k + 1)
                        if k >= 1:
                            act.wait_ge(sm["scanned" if i == 0 else "ld_lo_made"], k)
                        for m in range(KT):
                            last = a.activation(dst[:, m, :], src[:, m, :], ACT.Tanh, bias=hb[:, i, m:m + 1], scale=0.5)
                        last.then_inc(sm[made], 1)
                    if k < 2:
                        for b in (2 * k, 2 * k + 1):
                            act.wait_ge(gram_done, b + 1)
                            a.copy(gram_hi[:, b], (psS, psM)[b % 2]).then_inc(gram_hi_made, 1)
                    if k >= 1:
                        act.wait_ge(sm["o_done"], k)
                    act.wait_ge(sm["loaded"], k + 1)
                    a.copy(ld_hi[:, :, :], tq[:, :, :]).then_inc(sm["ld_hi_made"], 1)
                if 0 <= k - 3 < B:
                    act.wait_ge(sm["mx_made"], k - 2)
                    a.activation(sct[:, :], mx[:, :], ACT.Tanh, scale=0.5).then_inc(sm["sct_made"], 1)
                if 0 <= k - 2 < B:
                    act.wait_ge(sm["nmr_made"], k - 1)
                    for i in range(TB):
                        last = a.activation(z[:, i, :], psS[:, i, :], ACT.Identity, bias=nmr[:, i:i + 1],
                                            scale=rstd[:, SIM, i:i + 1])
                    last.then_inc(sm["zn_made"], 1)
                if 0 <= k - 3 < B:
                    act.wait_ge(sm["shg_done"], k - 2)
                    if k >= 4:
                        act.wait_ge(sm["hs_lo_made"], k - 3)
                    a.activation(hs[:, :, :], psG, ACT.Tanh, scale=0.5).then_inc(sm["th_made"], 1)
                    act.wait_ge(sm["h_made"], k - 2)
                    if k >= 4:
                        act.wait_ge(sm["sd_done"], k - 3)
                    a.copy(hs_hi[:, :, :], hs[:, :, :]).then_inc(sm["hs_hi_made"], 1)
                if 0 <= k - 1 < B:
                    if k >= 2:
                        act.wait_ge(sm["sim_done"], k - 1)
                    evacuate_hi(psU, xT2_hi[:, :, :], "t2_done", k, "xT2_hi_made")
                if 0 <= k - 2 < B:
                    act.wait_ge(sm["max_made"], k - 1)
                    if k >= 3:
                        act.wait_ge(sm["x3_made"], k - 2)
                    for i in range(TB):
                        last = a.activation(ez[:, i, :], z[:, i, :], ACT.Exp, bias=nmax[:, i:i + 1],
                                            accum_out=ssum[:, i:i + 1])
                    last.then_inc(sm["exp_made"], 1)
                    if k >= 3:
                        act.wait_ge(sm["shu_done"], k - 2)
                    evacuate_hi(psU, xT3_hi[:, :, :], "t3_done", k - 1, "xT3_hi_made")
                for n in range(*PLAN[k]):
                    unit(n)

            def rows_hi(s, r, reused):
                act.wait_ge(tx_done, s + 1)
                if reused:
                    act.wait_ge(gu_done, s - 1)
                a.copy(xgT_hi[:, r], psX[r]).then_inc(xg_hi_made, 1)

            def gate_tanh(s, r, reused):
                act.wait_ge(gu_done, s + 1)
                if reused:
                    act.wait_ge(th_done, s - 1)
                a.activation(rh[:, r, :], psGU[r][:, 0:D], ACT.Tanh, scale=0.5).then_inc(rth_made, 1)

            def hidden_hi(s, r, reused):
                act.wait_ge(th_done, s + 1)
                if reused:
                    act.wait_ge(down_done, s - 1)
                a.copy(hT_hi[:, r], psH[r]).then_inc(hT_hi_made, 1)

            def result(s, r, stores):
                act.wait_ge(down_done, s + 1)
                act.wait_ge(y_out[r], 16 * stores)
                a.copy(ry[:, r, :], psY[r][:, 0, :]).then_inc(y_made, 1)

            rows_hi(0, 0, False)
            rows_hi(1, 1, False)
            gate_tanh(0, 0, False)
            for s in range(ROUTED_PEEL):
                gate_tanh(s + 1, (s + 1) % 2, s + 1 >= 2)
                hidden_hi(s, s % 2, s >= 2)
                if s >= 1:
                    result(s - 1, (s - 1) % 2, 0)
                rows_hi(s + 2, s % 2, True)
            with act.Fori(0, ROUTED_LOOPS) as i:
                for j in range(2):
                    s = i * 2 + (ROUTED_PEEL + j)
                    r = (ROUTED_PEEL + j) % 2
                    gate_tanh(s + 1, 1 - r, True)
                    hidden_hi(s, r, True)
                    result(s - 1, 1 - r, i + 1)
                    rows_hi(s + 2, r, True)
            for s in range(NS - 2, NS + 1):
                if s + 1 < NS:
                    gate_tanh(s + 1, (s + 1) % 2, True)
                if s < NS:
                    hidden_hi(s, s % 2, True)
                result(s - 1, (s - 1) % 2, (s - 1) // 2)

        @block.vector
        def _(dve):
            v = nc.vector
            v.memset(zero[:, :], 0.0)
            v.memset(onehot[:, NT, :], 0.0).then_inc(dve_consts, 1)
            v.memset(ones[:, :], 1.0)
            v.memset(one_e[:, :], 1.0)
            v.memset(decay[:, :], DECAY).then_inc(dve_consts, 1)

            def statistics(kind, b, tile):
                n = nth(kind, b)
                for i in range(TB):
                    last = v.bn_stats(bn[:, kind, i, :], tile(i))
                last.then_inc(bn_raw, 1)
                dve.wait_ge(bn_raw, n)
                for i in range(TB):
                    last = v.bn_aggr(mv[:, kind, i, :], bn[:, kind, i, :])
                last.then_inc(stats, 1)

            def normalise(kind, b, dst, tile, made):
                dve.wait_ge(rstd_made, nth(kind, b))
                for i in range(TB):
                    last = v.tensor_scalar(dst(i), tile(i), mv[:, kind, i, 0:1], rstd[:, kind, i:i + 1],
                                           ALU.subtract, ALU.mult)
                last.then_inc(sm[made], 1)

            def residual(b):
                return lambda i: res[:, b * TB + i, :]

            def lo_part(dst, src, hi, ready, count, made):
                dve.wait_ge(sm[ready], count)
                v.tensor_tensor(dst, src, f32(hi), ALU.subtract).then_inc(sm[made], 1)

            def ln1_stats(b):
                dve.wait_ge(x_in[b], 16)
                statistics(LN1, b, residual(b))

            def ln1_apply(b):
                if b >= 2:
                    dve.wait_ge(sm["t1_done"], b - 1)
                normalise(LN1, b, lambda i: xn1[:, b % 2, i, :], residual(b), "xn1_made")

            def memory(b):
                dve.wait_ge(sm["tg_made"], b + 1)
                dve.wait_ge(sm["v_done"], b + 1)
                v.scalar_tensor_tensor(tg[:, :, :], tg[:, :, :], 1.0, psV, ALU.add, ALU.mult).then_inc(sm["stored"], 1)
                dve.wait_ge(sm["stored"], b + 1)
                for m in range(KT):
                    last = v.tensor_tensor_scan(mem[:, m, :], decay[:, :], tg[:, m, :], 0.0, ALU.mult, ALU.add)
                last.then_inc(sm["scanned"], 1)
                dve.wait_ge(sm["scanned"], b + 1)
                dve.wait_ge(sm["tq_made"], b + 1)
                v.scalar_tensor_tensor(tq[:, :, :], tq[:, :, :], 1.0, mem[:, :, :], ALU.add, ALU.mult).then_inc(sm["loaded"], 1)

            def route_batch(b):
                n = b + 1
                dve.wait_ge(sm["lg_done"], n)
                v.tensor_copy(lg[:, :, :], ps_lg).then_inc(sm["lg_copied"], 1)
                dve.wait_ge(sm["lg_copied"], n)
                v.tensor_reduce(mx[:, :], lg[:, :, :], AX.X, ALU.max).then_inc(sm["mx_made"], 1)
                dve.wait_ge(sm["mx_made"], n)
                v.tensor_tensor(cand[:, :, :], lg[:, :, :], mx[:, :].unsqueeze(2).to_broadcast([P, TB, E]), ALU.is_equal).then_inc(sm["eq_made"], 1)
                dve.wait_ge(sm["eq_made"], n)
                v.tensor_tensor(cand[:, :, :], cand[:, :, :], io_e8[:, :, :], ALU.mult).then_inc(sm["cand_made"], 1)
                dve.wait_ge(sm["cand_made"], n)
                v.tensor_reduce(idx[:, :], cand[:, :, :], AX.X, ALU.min).then_inc(sm["idx_made"], 1)
                dve.wait_ge(sm["idx_made"], n)
                v.tensor_tensor(onehot[:, b * TB:(b + 1) * TB, :], io_e8[:, :, :],
                                idx[:, :].unsqueeze(2).to_broadcast([P, TB, E]), ALU.is_equal).then_inc(sm["onehot_made"], 1)
                dve.wait_ge(sm["sct_made"], n)
                v.tensor_scalar(score[:, :], sct[:, :], 0.5, 0.5, ALU.mult, ALU.add).then_inc(sm["score_made"], 1)
                dve.wait_ge(sm["score_made"], n)
                if b == 0:
                    dve.wait_ge(gram_done, B)
                for i in range(TB):
                    last = v.tensor_scalar(xs[:, b * TB + i, :], xn3[:, i, :], score[:, i:i + 1], None, ALU.mult)
                last.then_inc(sm["xs_made"], 1)

            def shared_hidden(b):
                dve.wait_ge(sm["th_made"], b + 1)
                v.scalar_tensor_tensor(hs[:, :, :], hs[:, :, :], 1.0, psG, ALU.add, ALU.mult).then_inc(sm["ht_made"], 1)
                dve.wait_ge(sm["ht_made"], b + 1)
                dve.wait_ge(sm["shu_done"], b + 1)
                v.tensor_tensor(hs[:, :, :], hs[:, :, :], psQ, ALU.mult).then_inc(sm["h_made"], 1)

            def shared_add(b):
                dve.wait_ge(sm["sd_done"], b + 1)
                v.scalar_tensor_tensor(res[:, b * TB:(b + 1) * TB, :], psV, 0.5, res[:, b * TB:(b + 1) * TB, :],
                                       ALU.mult, ALU.add).then_inc(sm["base_made"], 1)

            ln1_stats(0)
            ln1_apply(0)
            for k in range(STEPS):
                if k + 1 < B:
                    ln1_stats(k + 1)
                if k == 0:
                    dve.wait_ge(dve_consts, 2)
                if k == 1:
                    dve.wait_ge(rw_loaded, 16)
                    v.tensor_copy(rw_hi[:, :, :], rw[:, :, :]).then_inc(rw_split, 1)
                    dve.wait_ge(rw_split, 1)
                    v.tensor_tensor(rw_lo[:, :, :], rw[:, :, :], f32(rw_hi[:, :, :]), ALU.subtract).then_inc(rw_split, 1)
                if k < B:
                    lo_part(xT1_lo[:, k % 2], psT, xT1_hi[:, k % 2], "xT1_hi_made", k + 1, "xT1_lo_made")
                    if k + 1 < B:
                        ln1_apply(k + 1)
                    memory(k)
                if k < 2:
                    for b in (2 * k, 2 * k + 1):
                        dve.wait_ge(gram_hi_made, b + 1)
                        v.tensor_tensor(gram_lo[:, b], (psS, psM)[b % 2], f32(gram_hi[:, b]), ALU.subtract).then_inc(gram_lo_made, 1)
                if 0 <= k - 3 < B:
                    route_batch(k - 3)
                if 0 <= k - 1 < B:
                    b = k - 1
                    dve.wait_ge(sm["o_done"], b + 1)
                    v.scalar_tensor_tensor(res[:, b * TB:(b + 1) * TB, :], psO, MEM_SCALE, res[:, b * TB:(b + 1) * TB, :],
                                           ALU.mult, ALU.add).then_inc(sm["x2_made"], 1)
                    dve.wait_ge(sm["x2_made"], b + 1)
                    statistics(LN2, b, residual(b))
                    if b >= 1:
                        dve.wait_ge(sm["t2_done"], b)
                    normalise(LN2, b, lambda i: xn2[:, i, :], residual(b), "xn2_made")
                if 0 <= k - 2 < B:
                    b = k - 2
                    dve.wait_ge(sm["sim_done"], b + 1)
                    statistics(SIM, b, lambda i: psS[:, i, :])
                    dve.wait_ge(rstd_made, nth(SIM, b))
                    v.scalar_tensor_tensor(nmr[:, :], mv[:, SIM, :, 0], -1.0, rstd[:, SIM, :], ALU.mult, ALU.mult).then_inc(sm["nmr_made"], 1)
                if 0 <= k - 3 < B:
                    shared_hidden(k - 3)
                if 0 <= k - 1 < B:
                    lo_part(xT2_lo[:, :, :], psU, xT2_hi[:, :, :], "xT2_hi_made", k, "xT2_lo_made")
                if 0 <= k - 2 < B:
                    b = k - 2
                    dve.wait_ge(sm["z_made"], b + 1)
                    v.tensor_reduce(nmax[:, :], z[:, :, :], AX.X, ALU.max, negate=True).then_inc(sm["max_made"], 1)
                    dve.wait_ge(sm["exp_made"], b + 1)
                    v.reciprocal(rsum[:, :], ssum[:, :]).then_inc(sm["rsum_made"], 1)
                    dve.wait_ge(sm["rsum_made"], b + 1)
                    for i in range(TB):
                        t = b * TB + i
                        last = v.scalar_tensor_tensor(res[:, t, :], ez[:, i, :], rsum[:, i:i + 1], res[:, t, :],
                                                      ALU.mult, ALU.add)
                    last.then_inc(sm["x3_made"], 1)
                    dve.wait_ge(sm["x3_made"], b + 1)
                    statistics(LN3, b, residual(b))
                if 0 <= k - 3 < B:
                    shared_add(k - 3)
                if 0 <= k - 2 < B:
                    b = k - 2
                    if b >= 1:
                        dve.wait_ge(sm["t3_done"], b)
                    normalise(LN3, b, lambda i: xn3[:, i, :], residual(b), "xn3_made")
                    lo_part(xT3_lo[:, :, :], psU, xT3_hi[:, :, :], "xT3_hi_made", b + 1, "xT3_lo_made")
            dve.wait_ge(rank_done, 1)
            dve.wait_ge(consts_made, 1)
            step = [0]

            def link(ins):
                step[0] += 1
                ins.then_inc(route_step, 1)
                dve.wait_ge(route_step, step[0])

            link(v.tensor_tensor(cmp_k[:, :, :], io_k[:, :, :], count.unsqueeze(2).to_broadcast([P, E, NT]), ALU.is_lt))
            link(v.tensor_reduce(ntile[:, :], cmp_k[:, :, :], AX.X, ALU.add))
            link(v.tensor_tensor_scan(incl[:, :], one_e[:, :], ntile[:, :], 0.0, ALU.mult, ALU.add))
            link(v.tensor_tensor(excl[:, :], incl[:, :], ntile[:, :], ALU.subtract))
            link(v.scalar_tensor_tensor(slot_a[:, :, :], excl[:, :].unsqueeze(1).to_broadcast([P, NT, E]), float(P), rank, ALU.mult, ALU.add))
            link(v.tensor_tensor(slot_b[:, :, :], slot_a[:, :, :], onehot[:, 0:NT, :], ALU.mult))
            link(v.tensor_reduce(dest_f[:, :], slot_b[:, :, :], AX.X, ALU.add))
            v.tensor_copy(dest[:, :], dest_f[:, :]).then_inc(dest_made, 1)
            link(v.tensor_tensor(cmp_s[:, :, :], io_s[:, :, :], incl[0:1, :].unsqueeze(1).to_broadcast([1, NS, E]), ALU.is_ge))
            link(v.tensor_reduce(te_f[:, :], cmp_s[:, :, :], AX.X, ALU.add))
            v.tensor_scalar(te[:, :], te_f[:, :], float(E - 1), None, ALU.min).then_inc(te_made, 1)

            def hidden(s, r):
                dve.wait_ge(rth_made, s + 1)
                v.scalar_tensor_tensor(rh[:, r, :], rh[:, r, :], 1.0, psGU[r][:, 0:D], ALU.add, ALU.mult).then_inc(rt_made, 1)
                dve.wait_ge(rt_made, s + 1)
                v.tensor_tensor(rh[:, r, :], rh[:, r, :], psGU[r][:, D:2 * D], ALU.mult).then_inc(rh_made, 1)

            def rows_lo(s, r):
                dve.wait_ge(xg_hi_made, s + 1)
                v.tensor_tensor(xgT_lo[:, r], psX[r], f32(xgT_hi[:, r]), ALU.subtract).then_inc(xg_lo_made, 1)

            def hidden_lo(s, r):
                dve.wait_ge(hT_hi_made, s + 1)
                v.tensor_tensor(hT_lo[:, r], psH[r], f32(hT_hi[:, r]), ALU.subtract).then_inc(hT_lo_made, 1)

            rows_lo(0, 0)
            rows_lo(1, 1)
            hidden(0, 0)
            for s in range(ROUTED_PEEL):
                hidden(s + 1, (s + 1) % 2)
                hidden_lo(s, s % 2)
                rows_lo(s + 2, s % 2)
            with dve.Fori(0, ROUTED_LOOPS) as i:
                for j in range(2):
                    s = i * 2 + (ROUTED_PEEL + j)
                    r = (ROUTED_PEEL + j) % 2
                    hidden(s + 1, 1 - r)
                    hidden_lo(s, r)
                    rows_lo(s + 2, r)
            hidden(NS - 1, (NS - 1) % 2)
            hidden_lo(NS - 2, (NS - 2) % 2)
            hidden_lo(NS - 1, (NS - 1) % 2)
            for t in range(NT):
                dve.wait_ge(gathered[t], 16)
                last = v.scalar_tensor_tensor(res[:, t, :], xs[:, t, :], 0.5, res[:, t, :], ALU.mult, ALU.add)
                if t % TB == TB - 1:
                    last.then_inc(final_made, 1)

        @block.tensor
        def _(pe):
            T = nc.tensor

            def product(out_ap, pairs):
                terms = [(a, c) for a, _, c, _ in pairs] + [(b, c) for _, b, c, _ in pairs] + [(a, d) for a, _, _, d in pairs]
                for i, (l, r) in enumerate(terms):
                    last = T.matmul(out_ap, l, r, start=(i == 0), stop=(i == len(terms) - 1))
                return last

            def transposed(ps, rows_of, ready, count, done):
                pe.wait_ge(sm[ready], count)
                for i in range(TB):
                    for k in range(KT):
                        last = T.transpose(ps[:, k, i * P:(i + 1) * P], rows_of(i)[:, k * P:(k + 1) * P], ident[:, :])
                last.then_inc(sm[done], 1)

            def project(b, w, ps, done):
                for m in range(KT):
                    last = product(ps[:, m, :], [(gqvo_hi[:, w, k, m * P:(m + 1) * P], gqvo_lo[:, w, k, m * P:(m + 1) * P],
                                                  xT1_hi[:, b % 2, k, :], xT1_lo[:, b % 2, k, :]) for k in range(KT)])
                last.then_inc(sm[done], 1)

            def gram(b):
                kv = kvT[:, b * S:(b + 1) * S]
                for m in range(KT):
                    last = T.matmul((psS, psM)[b % 2][:, m, :], kv[:, m * P:(m + 1) * P], kv, start=True, stop=True)
                last.then_inc(gram_done, 1)

            def shared(b, w, ps, done):
                for m in range(KT):
                    last = product(ps[:, m, :], [(shw_hi[:, w, k, m * P:(m + 1) * P], shw_lo[:, w, k, m * P:(m + 1) * P],
                                                  xT3_hi[:, k, :], xT3_lo[:, k, :]) for k in range(KT)])
                last.then_inc(sm[done], 1)

            def shared_gate(b):
                pe.wait_ge(unit_lo, U_SG + 1)
                pe.wait_ge(sm["xT3_hi_made"], b + 1)
                pe.wait_ge(sm["xT3_lo_made"], b + 1)
                pe.wait_ge(sm["tg_made"], min(b + 4, B))
                shared(b, 0, psG, "shg_done")

            def shared_up(b):
                pe.wait_ge(unit_lo, U_SU + 1)
                pe.wait_ge(sm["tq_made"], min(b + 4, B))
                shared(b, 1, psQ, "shu_done")

            def shared_down(b):
                pe.wait_ge(unit_lo, U_SD + 1)
                pe.wait_ge(sm["hs_hi_made"], b + 1)
                pe.wait_ge(sm["hs_lo_made"], b + 1)
                pe.wait_ge(sm["stored"], min(b + 4, B))
                if b >= 1:
                    pe.wait_ge(sm["base_made"], b)
                for i in range(TB):
                    last = product(psV[:, i, :], [(hs_hi[:, k, i * P:(i + 1) * P], hs_lo[:, k, i * P:(i + 1) * P],
                                                   shw_hi[:, 2, k, :], shw_lo[:, 2, k, :]) for k in range(KT)])
                last.then_inc(sm["sd_done"], 1)

            pe.wait_ge(ident_made, 1)
            pe.wait_ge(small_loaded, 16 * SMALL)
            T.transpose(bS[0:C, 0:C], wk_nat[:, :], ident[0:C, 0:C]).then_inc(wk_t, 1)
            pe.wait_ge(ctx_loaded, 16)
            for h, b in enumerate((bO, bQ)):
                for t in range(NT // 2):
                    last = T.transpose(b[0:C, t * P:(t + 1) * P], ctx_nat[:, h * (NT // 2) + t, :], ident[:, :])
                last.then_inc(ctx_t, 1)
            for k in range(STEPS):
                if k < B:
                    if k >= 1:
                        pe.wait_ge(sm["xT1_hi_made"], k)
                        pe.wait_ge(sm["xT1_lo_made"], k)
                    transposed(psT, lambda i: xn1[:, k % 2, i, :], "xn1_made", k + 1, "t1_done")
                    if k == 0:
                        pe.wait_ge(ctxT_made, 2)
                        pe.wait_ge(wkT_made, 1)
                        for h, b in enumerate((bS, bM)):
                            T.matmul(b[0:C, :], wkT[:, :], ctxT[:, h * 512:(h + 1) * 512], start=True, stop=True).then_inc(kv_done, 1)
                    pe.wait_ge(unit_lo, U_V + 1)
                    pe.wait_ge(sm["xT1_hi_made"], k + 1)
                    pe.wait_ge(sm["xT1_lo_made"], k + 1)
                    if k >= 1:
                        pe.wait_ge(sm["tg_made"], k)
                    project(k, U_G, psG, "g_done")
                    if k >= 1:
                        pe.wait_ge(sm["tq_made"], k)
                    project(k, U_Q, psQ, "q_done")
                    if k >= 1:
                        pe.wait_ge(sm["stored"], k)
                    project(k, U_V, psV, "v_done")
                    if k < 2:
                        pe.wait_ge(kvT_made, 2)
                        for b in (2 * k, 2 * k + 1):
                            if b >= 2:
                                pe.wait_ge(gram_hi_made, b - 1)
                                pe.wait_ge(gram_lo_made, b - 1)
                            gram(b)
                if 0 <= k - 1 < B:
                    b = k - 1
                    pe.wait_ge(unit_lo, U_O + 1)
                    pe.wait_ge(sm["ld_hi_made"], b + 1)
                    pe.wait_ge(sm["ld_lo_made"], b + 1)
                    if b >= 1:
                        pe.wait_ge(sm["x2_made"], b)
                    for i in range(TB):
                        last = product(psO[:, i, :], [(ld_hi[:, m, i * P:(i + 1) * P], ld_lo[:, m, i * P:(i + 1) * P],
                                                       gqvo_hi[:, U_O, m, :], gqvo_lo[:, U_O, m, :]) for m in range(KT)])
                    last.then_inc(sm["o_done"], 1)
                if 0 <= k - 2 < B:
                    b = k - 2
                    pe.wait_ge(gram_hi_made, B)
                    pe.wait_ge(gram_lo_made, B)
                    pe.wait_ge(sm["xT2_hi_made"], b + 1)
                    pe.wait_ge(sm["xT2_lo_made"], b + 1)
                    if b >= 1:
                        pe.wait_ge(sm["zn_made"], b)
                    for i in range(TB):
                        last = product(psS[:, i, :], [(xT2_hi[:, m, i * P:(i + 1) * P], xT2_lo[:, m, i * P:(i + 1) * P],
                                                       gram_hi[:, b, m, :], gram_lo[:, b, m, :]) for m in range(KT)])
                    last.then_inc(sm["sim_done"], 1)
                if 0 <= k - 3 < B:
                    shared_gate(k - 3)
                    shared_up(k - 3)
                if 0 <= k - 1 < B:
                    if k >= 3:
                        pe.wait_ge(sm["xT3_hi_made"], k - 2)
                        pe.wait_ge(sm["xT3_lo_made"], k - 2)
                    transposed(psU, lambda i: xn2[:, i, :], "xn2_made", k, "t2_done")
                if 0 <= k - 3 < B:
                    shared_down(k - 3)
                if 0 <= k - 2 < B:
                    b = k - 2
                    pe.wait_ge(sm["xT2_hi_made"], min(b + 2, B))
                    pe.wait_ge(sm["xT2_lo_made"], min(b + 2, B))
                    transposed(psU, lambda i: xn3[:, i, :], "xn3_made", b + 1, "t3_done")
                    if b == 0:
                        pe.wait_ge(rw_split, 2)
                    else:
                        pe.wait_ge(sm["lg_copied"], b)
                    pe.wait_ge(sm["xT3_hi_made"], b + 1)
                    pe.wait_ge(sm["xT3_lo_made"], b + 1)
                    for i in range(TB):
                        last = product(ps_lg[:, i, :], [(xT3_hi[:, k2, i * P:(i + 1) * P], xT3_lo[:, k2, i * P:(i + 1) * P],
                                                         rw_hi[:, k2, :], rw_lo[:, k2, :]) for k2 in range(KT)])
                    last.then_inc(sm["lg_done"], 1)
            pe.wait_ge(sm["onehot_made"], B)
            pe.wait_ge(consts_made, 1)
            pe.wait_ge(dve_consts, 2)
            T.matmul(ps_rank, below[:, :], onehot[:, :, :], start=True, stop=False)
            for d in range(1, NT + 1):
                last = T.matmul(ps_rank[:, d:NT + 1, :], ones[:, :], onehot[:, 0:NT + 1 - d, :], start=False, stop=(d == NT))
            last.then_inc(rank_done, 1)

            def rows_transposed(s, r, loads, reused):
                pe.wait_ge(xg_in[r], 16 * loads)
                if reused:
                    pe.wait_ge(xg_lo_made, s - 1)
                for k in range(KT):
                    last = T.transpose(psX[r][:, k, :], xg[:, r, k * P:(k + 1) * P], ident[:, :])
                last.then_inc(tx_done, 1)

            def gate_up(s, r, reused):
                e = T.value_load(te[0:1, bass.ds(s, 1)], min_val=0, max_val=E - 1)
                pe.wait_ge(xg_lo_made, s + 1)
                if reused:
                    pe.wait_ge(rh_made, s - 1)
                product(psGU[r][:, :], [(xgT_hi[:, r, k, :], xgT_lo[:, r, k, :], gu_hi[:, e, k, :], gu_lo[:, e, k, :])
                                        for k in range(KT)]).then_inc(gu_done, 1)

            def hidden_transposed(s, r, reused):
                pe.wait_ge(rh_made, s + 1)
                if reused:
                    pe.wait_ge(hT_lo_made, s - 1)
                for k in range(KT):
                    last = T.transpose(psH[r][:, k, :], rh[:, r, k * P:(k + 1) * P], ident[:, :])
                last.then_inc(th_done, 1)

            def down(s, r, reused):
                e = T.value_load(te[0:1, bass.ds(s, 1)], min_val=0, max_val=E - 1)
                pe.wait_ge(hT_lo_made, s + 1)
                if reused:
                    pe.wait_ge(y_made, s - 1)
                product(psY[r][:, 0, :], [(hT_hi[:, r, k, :], hT_lo[:, r, k, :], dn_hi[:, e, k, :], dn_lo[:, e, k, :])
                                          for k in range(KT)]).then_inc(down_done, 1)

            pe.wait_ge(te_made, 1)
            pe.wait_ge(unit_lo, len(units))
            pe.wait_ge(sm["h_made"], B)
            pe.wait_ge(sm["base_made"], B)
            pe.wait_ge(dest_made, 1)
            rows_transposed(0, 0, 1, False)
            rows_transposed(1, 1, 1, False)
            gate_up(0, 0, False)
            for s in range(ROUTED_PEEL):
                gate_up(s + 1, (s + 1) % 2, s + 1 >= 2)
                hidden_transposed(s, s % 2, s >= 2)
                if s >= 1:
                    down(s - 1, (s - 1) % 2, False)
                rows_transposed(s + 2, s % 2, s // 2 + 2, True)
            with pe.Fori(0, ROUTED_LOOPS) as i:
                for j in range(2):
                    s = i * 2 + (ROUTED_PEEL + j)
                    r = (ROUTED_PEEL + j) % 2
                    gate_up(s + 1, 1 - r, True)
                    hidden_transposed(s, r, True)
                    down(s - 1, 1 - r, True)
                    rows_transposed(s + 2, r, i + ((ROUTED_PEEL + j) // 2 + 2), True)
            for s in range(NS - 2, NS + 1):
                if s + 1 < NS:
                    gate_up(s + 1, (s + 1) % 2, True)
                if s < NS:
                    hidden_transposed(s, s % 2, True)
                down(s - 1, (s - 1) % 2, True)


_INS = ["x", "ctx_512", "L0_attn_Wv", "L0_attn_Wg", "L0_attn_bg", "L0_attn_Wq", "L0_attn_bq", "L0_attn_Wo",
        "L0_xattn_W_k", "L0_xattn_b_k", "L0_xattn_ln_gamma", "L0_xattn_ln_beta", "L0_ffn_router_w",
        "L0_ffn_gate_w", "L0_ffn_up_w", "L0_ffn_down_w", "L0_ffn_shared_gate_w", "L0_ffn_shared_up_w",
        "L0_ffn_shared_down_w"]


def kernel(**inputs):
    import numpy as _np
    import concourse.bacc as _bacc
    from concourse import mybir as _mybir
    from concourse.bass_utils import run_bass_kernel_spmd as _run

    nc = _bacc.Bacc("TRN2", target_bir_lowering=False, num_devices=1)
    arrays, args = {}, []
    for name in _INS:
        a = _np.ascontiguousarray(inputs[name])
        arrays[f"in_{name}_dram"] = a
        args.append(nc.dram_tensor(f"in_{name}_dram", a.shape, _mybir.dt.from_np(a.dtype), kind="ExternalInput").ap())
    shape = inputs["x"].shape
    args.append(nc.dram_tensor("out_0_dram", shape, _mybir.dt.float32, kind="ExternalOutput").ap())
    decoder_kernel(nc, *args)
    r = _run(nc, [arrays], core_ids=[0])
    return r.results[0]["out_0_dram"]
```

```python
from contextlib import ExitStack

import concourse.bass as bass
from concourse import mybir
from concourse.alu_op_type import AluOpType as ALU

ACT = mybir.ActivationFunctionType
AX = mybir.AxisListType
F32 = mybir.dt.float32
F32R = mybir.dt.float32r
BF16 = mybir.dt.bfloat16
U32 = mybir.dt.uint32
I32 = mybir.dt.int32

P = 128
LN_EPS = 1e-5
SIM_EPS = 1e-6
DECAY = 0.95

PE_ORDER = """
    turn1:0 turn_ctx:1 turn_wk:0 turn_ctx:0 query:0 gate:0 value:0 kv:0 turn1:1 kv:1 recall:0
    query:1 gate:1 value:1 gram:0 turn1:2 turn2:0 gram:1 similarity:0 recall:1 gate:2 query:2
    value:2 gram:2 turn1:3 turn2:1 gram:3 recall:2 similarity:1 gate:3 query:3 turn3:0 value:3
    turn2:2 router:0 shared_gate:0 router_turn:0 similarity:2 recall:3 shared_up:0 rank:0 turn3:1
    shared_down:0 turn2:3 router:1 shared_up:1 router_turn:1 similarity:3 shared_gate:1 rank:1
    turn3:2 shared_down:1 router:2 shared_gate:2 router_turn:2 shared_up:2 rank:2 shared_down:2
    turn3:3 router:3 shared_up:3 router_turn:3 shared_gate:3 rank:3 shared_down:3
""".split()

ACT_ORDER = """
    weight_hi:0 weight_hi:1 weight_hi:2 turned1_hi:0 turned_ctx:1 turned_wk:0 turned_ctx:0 norm1:1
    weight_hi:3 query_tanh:0 norm1:2 gate_tanh:0 weight_hi:4 weight_hi:5 kv_bias:0 turned1_hi:1
    norm1:3 kv_bias:1 weight_hi:6 weight_hi:7 weight_hi:8 weight_hi:9 query_tanh:1 weight_hi:10
    gate_tanh:1 weight_hi:11 norm2:0 gram_copy:0 turned1_hi:2 turned2:0 weight_hi:12 gram_copy:1
    weight_hi:13 weight_hi:14 weight_hi:15 gate_tanh:2 weight_hi:16 query_tanh:2 softmax_exp:0
    norm2:1 gram_copy:2 turned1_hi:3 turned2:1 weight_hi:17 gram_copy:3 weight_hi:18 weight_hi:19
    weight_hi:20 weight_hi:21 norm3:0 gate_tanh:3 query_tanh:3 turned3_hi:0 norm2:2 softmax_exp:1
    weight_hi:22 router_copy:0 turned2:2 weight_hi:23 shared_tanh:0 weight_hi:24 weight_hi:25
    score_tanh:0 weight_hi:26 weight_hi:27 norm3:1 turned3_hi:1 norm2:3 softmax_exp:2 turned2:3
    weight_hi:28 router_copy:1 score_tanh:1 shared_tanh:1 norm3:2 turned3_hi:2 softmax_exp:3
    router_copy:2 shared_tanh:2 score_tanh:2 norm3:3 turned3_hi:3 router_copy:3 score_tanh:3
    shared_tanh:3
""".split()

DVE_ORDER = """
    stats1:0 weight_lo:0 weight_lo:1 norm1:0 weight_lo:2 stats1:1 turned1_lo:0 stats1:2 stats1:3
    memory:0 turned1_lo:1 residual2:0 memory:1 turned1_lo:2 sim_stats:0 sim_centre:0 residual2:1
    sim_scale:0 memory:2 residual3:0 turned1_lo:3 residual2:2 sim_stats:1 sim_centre:1 sim_scale:1
    turned3_lo:0 memory:3 residual3:1 route:0 sim_stats:2 residual2:3 sim_centre:2 shared_hidden:0
    sim_scale:2 turned3_lo:1 destination:0 shared_add:0 residual3:2 route:1 sim_stats:3 sim_centre:3
    destination:1 shared_hidden:1 sim_scale:3 turned3_lo:2 shared_add:1 residual3:3 route:2
    shared_hidden:2 destination:2 shared_add:2 turned3_lo:3 route:3 destination:3 shared_hidden:3
    slot_table:3 shared_add:3
""".split()

POOL_ORDER = """
    rstd1:0 rstd1:1 rstd1:2 rstd1:3 weight_lo:3 weight_lo:4 weight_lo:5 weight_lo:6 weight_lo:7
    rstd2:0 weight_lo:8 weight_lo:9 weight_lo:10 weight_lo:11 weight_lo:12 sim_rstd:0 weight_lo:13
    rstd2:1 weight_lo:14 weight_lo:15 weight_lo:16 weight_lo:17 rstd3:0 weight_lo:18 sim_rstd:1
    rstd2:2 weight_lo:19 weight_lo:20 weight_lo:21 weight_lo:22 rstd3:1 weight_lo:23 scale_rows:0
    sim_rstd:2 rstd2:3 weight_lo:24 weight_lo:25 scatter:0 weight_lo:26 rstd3:2 scale_rows:1
    sim_rstd:3 scatter:1 weight_lo:27 weight_lo:28 rstd3:3 scale_rows:2 scatter:2 scale_rows:3
    scatter:3
""".split()


def steps_of(order):
    for item in order:
        name, _, n = item.partition(":")
        yield name, int(n)


def decoder_kernel(nc, x, ctx_in, Wv, Wg, bg, Wq, bq, Wo, W_k, b_k, gamma, beta,
                   router_w, gate_w, up_w, down_w, sh_gate_w, sh_up_w, sh_down_w, out):
    B, S, D = x.shape
    C = ctx_in.shape[2]
    E = router_w.shape[1]
    KT = D // P
    TB = S // P
    NT = B * TB
    N = B * S
    NS = (N + E * (P - 1)) // P
    REGION = N + P
    W = D + 16
    NOWHERE = 1 << 20
    SIM_SCALE = float(D) ** -0.5
    MEM_SCALE = 0.25 * (1.0 - DECAY)
    PEEL = 3
    LOOPS = (NS - 3 - PEEL) // 2
    REST = PEEL + 2 * LOOPS
    RING = 4
    PROJ = 3

    x_sorted = nc.dram_tensor("x_sorted", (E * REGION + P, W), F32, kind="Internal").ap()
    base_rows = nc.dram_tensor("base_rows", (N, D), F32, kind="Internal").ap()
    out_rows = out.rearrange("b s d -> (b s) d")

    with ExitStack() as ctx:
        def sb(name, shape, dt=F32):
            return ctx.enter_context(nc.sbuf_tensor(name, shape, dt))

        def bank(name):
            return ctx.enter_context(nc.psum_tensor(name, [P, 512], F32))

        def sem(name):
            return ctx.enter_context(nc.semaphore(name))

        res = sb("res", [P, NT, D])
        xs = sb("xs", [P, NT, W])
        xn1 = sb("xn1", [P, 2, TB, D])
        xn2 = sb("xn2", [P, TB, D])
        xn3 = sb("xn3", [P, TB, D])
        xT1_hi = sb("xT1_hi", [P, 2, KT, S], F32R)
        xT1_lo = sb("xT1_lo", [P, 2, KT, S], F32R)
        xT2 = sb("xT2", [P, 2, KT, S])
        xT3_hi = sb("xT3_hi", [P, 2, KT, S], F32R)
        xT3_lo = sb("xT3_lo", [P, 2, KT, S], F32R)
        gqv_hi = sb("gqv_hi", [P, PROJ, KT, D], F32R)
        gqv_lo = sb("gqv_lo", [P, PROJ, KT, D], F32R)
        wo = sb("wo", [P, KT, D])
        shw_hi = sb("shw_hi", [P, 2, KT, D], F32R)
        shw_lo = sb("shw_lo", [P, 2, KT, D], F32R)
        shd = sb("shd", [P, KT, D])
        gu_hi = sb("gu_hi", [P, E, KT, 2 * D], F32R)
        gu_lo = sb("gu_lo", [P, E, KT, 2 * D], F32R)
        dn_hi = sb("dn_hi", [P, E, KT, D], F32R)
        dn_lo = sb("dn_lo", [P, E, KT, D], F32R)
        gram = sb("gram", [P, B, KT, S])
        stage = sb("stage", [P, RING, KT, D])
        tg = sb("tg", [P, KT, S])
        tq = sb("tq", [P, 2, KT, S])
        mem = sb("mem", [P, 2, W])
        z = sb("z", [P, TB, S])
        ez = sb("ez", [P, TB, S])
        hs = sb("hs", [P, 2, KT, S])
        ctx_nat = ez[:, :, :].rearrange("p i (t c) -> p (i t) c", c=C)
        wk_nat = sb("wk_nat", [C, C])
        wkT = sb("wkT", [C, C])
        bk = sb("bk", [C, 1])
        hb = sb("hb", [P, 2, KT])
        gam = sb("gam", [P, S])
        bet = sb("bet", [P, S])
        decay = sb("decay", [P, S])
        pad = sb("pad", [P, W])
        ident = sb("ident", [P, P])
        below = sb("below", [P, P], BF16)
        ones = sb("ones", [P, P], BF16)
        expo = sb("expo", [P, TB])
        rw = sb("rw", [P, KT, E])
        rw_hi = sb("rw_hi", [P, KT, E], F32R)
        rw_lo = sb("rw_lo", [P, KT, E], F32R)
        lgT = sb("lgT", [E, S])
        io_e8 = sb("io_e8", [P, TB, E])
        io_reg = sb("io_reg", [P, TB, E])
        io_k = sb("io_k", [P, E, NT])
        io_s = sb("io_s", [1, NS])
        bn = sb("bn", [P, 4, B, TB, 6])
        mv = sb("mv", [P, 4, B, TB, 2])
        vareps = sb("vareps", [P, 4, B, TB])
        rstd = sb("rstd", [P, 4, B, TB])
        shift = sb("shift", [P, 4, B, TB])
        nmax = sb("nmax", [P, B, TB])
        ssum = sb("ssum", [P, B, TB])
        rsum = sb("rsum", [P, B, TB])
        lg = sb("lg", [P, TB, E])
        mx = sb("mx", [P, B, TB])
        sct = sb("sct", [P, B, TB])
        score = sb("score", [P, B, TB])
        cand = sb("cand", [P, TB, E])
        idx = sb("idx", [P, TB])
        onehot = sb("onehot", [P, NT, E], BF16)
        row_e = sb("row_e", [P, TB, E])
        dest_f = sb("dest_f", [P, NT])
        dest = sb("dest", [P, NT], U32)
        cmp_k = sb("cmp_k", [1, E, NT])
        ntile = sb("ntile", [1, E])
        one_e = sb("one_e", [1, E])
        incl = sb("incl", [1, E])
        tile_s = sb("tile_s", [1, NS])
        cmp_s = sb("cmp_s", [1, NS, E])
        te_f = sb("te_f", [1, NS])
        before = sb("before", [1, NS])
        tr_f = sb("tr_f", [1, NS])
        te = sb("te", [1, NS], I32)
        tr = sb("tr", [1, NS], I32)
        cnt = sb("cnt", [1, E], I32)
        tid = sb("tid", [P, NS], U32)
        xg = mem
        xgT_hi, xgT_lo = xT1_hi[:, :, :, 0:P], xT1_lo[:, :, :, 0:P]
        hT_hi, hT_lo = xT1_hi[:, :, :, P:2 * P], xT1_lo[:, :, :, P:2 * P]
        rh = tg
        rb = tq[:, 0]
        ry = z

        bT, bU, bG, bQ, bV, bO, bS, bM = [bank(n) for n in ("bT", "bU", "bG", "bQ", "bV", "bO", "bS", "bM")]

        def halves(b):
            return b[:, :].rearrange("p (k n) -> p k n", k=2)

        psT, psU, psG, psQ, psV, psO, psS, psM = [halves(b) for b in (bT, bU, bG, bQ, bV, bO, bS, bM)]
        ps_lgT = bM[0:E, 0:S]
        ps_lg = bM[:, S:S + TB * E].rearrange("p (t e) -> p t e", e=E)
        ps_rank = bT[:, 0:TB * E].rearrange("p (t e) -> p t e", e=E)
        ps_count = bT[:, TB * E:TB * E + E]
        psX, psH, psGU, psY = [psT, psS], [psU, psM], [bG, bQ], [psV, psO]

        x_in = [sem(f"x_in{b}") for b in range(B)]
        small_in = {n: sem(f"{n}_in") for n in ("wk", "ctx", "bk", "bias", "wo", "gamma", "beta", "rw", "shd")}
        stage_in = [sem(f"stage_in{r}") for r in range(RING)]
        unit_hi, proj_lo, unit_lo = sem("unit_hi"), sem("proj_lo"), sem("unit_lo")
        ident_raw, ident_made, below_raw, consts_made = sem("ident_raw"), sem("ident_made"), sem("below_raw"), sem("consts_made")
        dve_consts, rows_raw, rows_ready, pad_made = sem("dve_consts"), sem("rows_raw"), sem("rows_ready"), sem("pad_made")
        half_bias, rw_split = sem("half_bias"), sem("rw_split")
        KINDS = LN1, LN2, SIM, LN3 = range(4)
        bn_raw, stats, eps_added, rstd_made, negated, shift_made = ([sem(f"{n}{kind}") for kind in KINDS] for n in
                                                           ("bn_raw", "stats", "eps_added", "rstd_made", "negated", "shift_made"))
        names = ("xn1_made", "t1_done", "xT1_hi_made", "xT1_lo_made", "g_done", "q_done", "v_done",
                 "tg_made", "tq_made", "stored", "scanned", "loaded", "o_done",
                 "x2_made", "xn2_made", "t2_done", "xT2_made", "sim_done", "centred",
                 "z_made", "max_made", "exp_made", "rsum_made", "x3_made", "xn3_made",
                 "t3_done", "xT3_hi_made", "xT3_lo_made", "lgT_done", "lgT_copied", "lg_done", "lg_copied",
                 "mx_made", "sct_made", "score_made", "xs_made", "eq_made", "cand_made", "idx_made", "onehot_made",
                 "rank_done", "row_made", "row_picked", "dest_summed", "dest_made",
                 "shg_done", "shu_done", "th_made", "ht_made", "h_made", "sd_done", "base_made")
        sm = {n: sem(n) for n in names}
        wk_t, wkT_made = sem("wk_t"), sem("wkT_made")
        ctx_t, ctxT_made, kv_done, kvT_made = ([sem(f"{n}{h}") for h in range(2)]
                                               for n in ("ctx_t", "ctxT_made", "kv_done", "kvT_made"))
        gram_done, gram_made = sem("gram_done"), sem("gram_made")
        table_step, counts_made, table_made = sem("table_step"), sem("counts_made"), sem("table_made")
        base_out, padded, scattered = sem("base_out"), sem("padded"), sem("scattered")
        xg_in, rb_in = [sem("xg_in0"), sem("xg_in1")], [sem("rb_in0"), sem("rb_in1")]
        tid_made = sem("tid_made")
        tx_done, xg_hi_made, xg_lo_made = sem("tx_done"), sem("xg_hi_made"), sem("xg_lo_made")
        gu_done, rth_made, rt_made, rh_made = sem("gu_done"), sem("rth_made"), sem("rt_made"), sem("rh_made")
        th_done, hT_hi_made, hT_lo_made = sem("th_done"), sem("hT_hi_made"), sem("hT_lo_made")
        down_done, y_made = sem("down_done"), sem("y_made")
        written = [sem("written0"), sem("written1")]

        def rows(w):
            return w.rearrange("(k p) n -> p k n", p=P)

        units = [(rows(w), gqv_hi[:, i], gqv_lo[:, i]) for i, w in enumerate((Wg, Wq, Wv))]
        units += [(rows(w), shw_hi[:, i], shw_lo[:, i]) for i, w in enumerate((sh_gate_w, sh_up_w))]
        for e in range(E):
            units += [(rows(gate_w[e]), gu_hi[:, e, :, 0:D], gu_lo[:, e, :, 0:D]),
                      (rows(up_w[e]), gu_hi[:, e, :, D:2 * D], gu_lo[:, e, :, D:2 * D]),
                      (rows(down_w[e]), dn_hi[:, e], dn_lo[:, e])]
        SHARED_LO = 2

        def f32(ap):
            return ap.bitcast(F32)

        def ctxT(b):
            return xs[0:C, b, 0:S]

        def kvT(b):
            return xs[0:C, B + b, 0:S]

        def pad_regions(queue, engine, first, last):
            _, count = nc.values_load_multi_w_load_instructions(
                cnt[0:1, first:last], engines=[engine], min_val=0, max_val=N,
                skip_runtime_bounds_check_because="a count of tokens is at most all of them")
            for e in range(first, last):
                queue.dma_start(x_sorted[bass.ds(count[e - first] + e * REGION, P), :], pad[:, :]).then_inc(padded, 16)

        block = ctx.enter_context(nc.Block())

        @block.sync
        def _(sp):
            def load_x(b):
                sp.dma_start(res[:, b * TB:(b + 1) * TB, :], x[b].rearrange("(t p) d -> p t d", p=P)).then_inc(x_in[b], 16)

            def load_unit(n):
                if n >= RING:
                    old = n - RING
                    sp.wait_ge(unit_hi, old + 1)
                    if old < PROJ:
                        sp.wait_ge(proj_lo, old + 1)
                    else:
                        sp.wait_ge(unit_lo, old - PROJ + 1)
                sp.dma_start(stage[:, n % RING], units[n][0]).then_inc(stage_in[n % RING], 16)

            def load(name, dst, src, scattered_words=False):
                sp.dma_start(dst, src, allow_slow_non_contiguous=scattered_words).then_inc(small_in[name], 16)

            load_x(0)
            load_unit(0)
            load_unit(1)
            load_unit(2)
            load("ctx", ctx_nat, ctx_in.rearrange("b (t p) c -> p (b t) c", p=P))
            load("wk", wk_nat[:, :], W_k)
            load("bias", hb[:, 0, :], bg.rearrange("(m p) -> p m", p=P), True)
            load("bias", hb[:, 1, :], bq.rearrange("(m p) -> p m", p=P), True)
            load("bk", bk[:, :], b_k.rearrange("(p o) -> p o", o=1))
            load_x(1)
            load("wo", wo[:, :, :], rows(Wo))
            load_x(2)
            load_x(3)
            load("gamma", gam[:, :], gamma.unsqueeze(0).to_broadcast([P, S]))
            load("beta", bet[:, :], beta.unsqueeze(0).to_broadcast([P, S]))
            load("rw", rw[:, :, :], router_w.rearrange("(k p) e -> p k e", p=P))
            for n in range(PROJ, len(units)):
                load_unit(n)
                if n == RING:
                    load("shd", shd[:, :, :], rows(sh_down_w))

            def store_base(b):
                sp.wait_ge(sm["base_made"], b + 1)
                sp.dma_start(base_rows[b * S:(b + 1) * S, :].rearrange("(t p) d -> p t d", p=P),
                             res[:, b * TB:(b + 1) * TB, :]).then_inc(base_out, 16)

            for b in range(B - 1):
                store_base(b)
            sp.wait_ge(pad_made, 1)
            sp.dma_start(x_sorted[E * REGION:E * REGION + P, :], pad[:, :]).then_inc(padded, 16)
            sp.wait_ge(counts_made, 1)
            pad_regions(sp, mybir.EngineType.SP, 0, E // 2)
            store_base(B - 1)

            def first_rows(s, n):
                _, values = nc.values_load_multi_w_load_instructions(
                    tr[0:1, bass.ds(s, n)], engines=[mybir.EngineType.SP], min_val=0, max_val=E * REGION,
                    skip_runtime_bounds_check_because="slot_table's rows start a tile of a region or the padding behind them")
                return values

            def load_rows(r, row):
                sp.dma_start(xg[:, r, :], x_sorted[bass.ds(row, P), :]).then_inc(xg_in[r], 16)

            sp.wait_ge(table_made, 1)
            sp.wait_ge(padded, 16 * (E + 1))
            sp.wait_ge(scattered, 16 * NT)
            row = first_rows(0, 2)
            load_rows(0, row[0])
            load_rows(1, row[1])
            with sp.Fori(0, (NS - 3) // 2) as i:
                row = first_rows(i * 2 + 2, 2)
                for r in range(2):
                    sp.wait_ge(tx_done, i * 2 + (r + 1))
                    sp.wait_ge(tid_made, i * 2 + (r + 1))
                    load_rows(r, row[r])
            sp.wait_ge(tx_done, NS - 2)
            sp.wait_ge(tid_made, NS - 2)
            load_rows((NS - 1) % 2, first_rows(NS - 1, 1)[0])

        @block.gpsimd
        def _(pool):
            g = nc.gpsimd
            g.memset(ident[:, :], 0.0).then_inc(ident_raw, 1)
            g.memset(expo[:, :], -0.5).then_inc(ident_raw, 1)
            pool.wait_ge(ident_raw, 2)
            g.affine_select(out=ident[:, :], in_=ident[:, :], compare_op=ALU.not_equal, fill=1.0, base=0,
                            pattern=[[-1, P]], channel_multiplier=1).then_inc(ident_made, 1)
            g.memset(below[:, :], 1.0).then_inc(below_raw, 1)
            g.iota(io_e8[:, :, :], [[0, TB], [1, E]], -E, 0, True)
            g.iota(io_reg[:, :, :], [[0, TB], [REGION, E]], 0, 0, True)
            g.iota(io_k[:, :, :], [[0, E], [P, NT]], 0, 0, True)
            g.iota(io_s[:, :], [[1, NS]], 0, 0, True)
            g.memset(xs[:, :, D:W], 0.0).then_inc(rows_raw, 1)
            pool.wait_ge(rows_raw, 1)
            g.iota(xs[:, :, D:D + 1].bitcast(U32), [[P, NT], [1, 1]], 0, 1, True).then_inc(rows_ready, 1)
            pool.wait_ge(below_raw, 1)
            g.affine_select(out=below[:, :], in_=below[:, :], compare_op=ALU.is_gt, fill=0.0, base=0,
                            pattern=[[1, P]], channel_multiplier=-1).then_inc(consts_made, 1)

            def rsqrt(kind, b):
                eps = SIM_EPS / SIM_SCALE ** 2 if kind == SIM else LN_EPS
                pool.wait_ge(stats[kind], b + 1)
                g.tensor_scalar(vareps[:, kind, b, :], mv[:, kind, b, :, 1], eps, None, ALU.add).then_inc(eps_added[kind], 1)
                if kind != SIM and (kind, b) != (LN1, 0):
                    g.tensor_scalar(shift[:, kind, b, :], mv[:, kind, b, :, 0], -1.0, None, ALU.mult).then_inc(negated[kind], 1)
                pool.wait_ge(eps_added[kind], b + 1)
                g.tensor_tensor(rstd[:, kind, b, :], vareps[:, kind, b, :], expo[:, :], ALU.pow).then_inc(rstd_made[kind], 1)
                if kind != SIM and (kind, b) != (LN1, 0):
                    pool.wait_ge(negated[kind], b + 1 if kind != LN1 else b)
                    pool.wait_ge(rstd_made[kind], b + 1)
                    g.tensor_tensor(shift[:, kind, b, :], shift[:, kind, b, :], rstd[:, kind, b, :],
                                    ALU.mult).then_inc(shift_made[kind], 1)

            def scale_rows(b):
                pool.wait_ge(sm["sct_made"], b + 1)
                g.tensor_scalar(score[:, b, :], sct[:, b, :], 0.5, 0.5, ALU.mult, ALU.add).then_inc(sm["score_made"], 1)
                pool.wait_ge(sm["score_made"], b + 1)
                if b == 0:
                    pool.wait_ge(gram_done, B)
                for i in range(TB):
                    last = g.tensor_scalar(xs[:, b * TB + i, 0:D], xn3[:, i, :], score[:, b, i:i + 1], 1.0, ALU.mult, ALU.mult)
                last.then_inc(sm["xs_made"], 1)

            def scatter(b):
                pool.wait_ge(sm["dest_made"], b + 1)
                pool.wait_ge(sm["xs_made"], b + 1)
                pool.wait_ge(rows_ready, 1)
                for t in range(b * TB, (b + 1) * TB):
                    g.indirect_dma_start(x_sorted, bass.IndirectOffsetOnAxis(dest[:, t:t + 1], 0), xs[:, t, :], None,
                                         bounds_check=E * REGION - 1, oob_is_err=False).then_inc(scattered, 16)

            def weight_lo(n):
                pool.wait_ge(unit_hi, n + 1)
                g.tensor_tensor(units[n][2], stage[:, n % RING], f32(units[n][1]), ALU.subtract).then_inc(unit_lo, 1)

            steps = {"rstd1": lambda b: rsqrt(LN1, b), "rstd2": lambda b: rsqrt(LN2, b),
                     "sim_rstd": lambda b: rsqrt(SIM, b), "rstd3": lambda b: rsqrt(LN3, b),
                     "scale_rows": scale_rows, "scatter": scatter, "weight_lo": weight_lo}
            for name, n in steps_of(POOL_ORDER):
                steps[name](n)

            def gather(s):
                pool.wait_ge(tid_made, s + 1)
                if s >= 2:
                    pool.wait_ge(y_made, s - 1)
                g.indirect_dma_start(rb[:, s % 2, :], None, base_rows, bass.IndirectOffsetOnAxis(tid[:, s:s + 1], 0),
                                     bounds_check=N - 1, oob_is_err=False).then_inc(rb_in[s % 2], 16)

            def write(s):
                pool.wait_ge(y_made, s + 1)
                g.indirect_dma_start(out_rows, bass.IndirectOffsetOnAxis(tid[:, s:s + 1], 0), ry[:, s % 2, :], None,
                                     bounds_check=N - 1, oob_is_err=False).then_inc(written[s % 2], 16)

            pool.wait_ge(base_out, 16 * B)
            gather(0)
            gather(1)
            for s in range(NS):
                write(s)
                if s + 2 < NS:
                    gather(s + 2)
            pool.wait_ge(written[0], 16 * ((NS + 1) // 2))
            pool.wait_ge(written[1], 16 * (NS // 2))

        @block.scalar
        def _(act):
            a = nc.scalar

            def normalise(kind, b, dst, made):
                act.wait_ge(shift_made[kind], b + 1 if kind != LN1 else b)
                for i in range(TB):
                    last = a.activation(dst[:, i, :], res[:, b * TB + i, :], ACT.Identity, bias=shift[:, kind, b, i:i + 1],
                                        scale=rstd[:, kind, b, i:i + 1])
                last.then_inc(sm[made], 1)

            def norm1(b):
                if b == 1:
                    act.wait_ge(sm["xn1_made"], 1)
                if b >= 2:
                    act.wait_ge(sm["t1_done"], b - 1)
                normalise(LN1, b, xn1[:, b % 2], "xn1_made")

            def norm2(b):
                if b >= 1:
                    act.wait_ge(sm["t2_done"], b)
                normalise(LN2, b, xn2, "xn2_made")

            def norm3(b):
                if b >= 1:
                    act.wait_ge(sm["t3_done"], b)
                    act.wait_ge(sm["xs_made"], b)
                normalise(LN3, b, xn3, "xn3_made")

            def weight_hi(n):
                act.wait_ge(stage_in[n % RING], 16 * (n // RING + 1))
                a.copy(units[n][1], stage[:, n % RING]).then_inc(unit_hi, 1)

            def turned_wk(_):
                act.wait_ge(wk_t, 1)
                a.copy(wkT[:, :], bM[0:C, 0:C]).then_inc(wkT_made, 1)

            def turned_ctx(h):
                act.wait_ge(ctx_t[h], 1)
                if h == 0:
                    act.wait_ge(rows_ready, 1)
                a.copy(xs[0:C, 2 * h:2 * h + 2, 0:S], (psO, psS)[h][0:C]).then_inc(ctxT_made[h], 1)

            def kv_bias(h):
                act.wait_ge(kv_done[h], 1)
                act.wait_ge(small_in["bk"], 16)
                a.activation(xs[0:C, B + 2 * h:B + 2 * h + 2, 0:S], (psU, psM)[h][0:C], ACT.Identity,
                             bias=bk[:, :]).then_inc(kvT_made[h], 1)

            def gram_copy(b):
                act.wait_ge(gram_done, b + 1)
                a.copy(gram[:, b], psM).then_inc(gram_made, 1)

            def turned1_hi(b):
                act.wait_ge(sm["t1_done"], b + 1)
                if b >= 2:
                    act.wait_ge(sm["g_done"], b - 1)
                    act.wait_ge(sm["q_done"], b - 1)
                    act.wait_ge(sm["v_done"], b - 1)
                a.copy(xT1_hi[:, b % 2], psT).then_inc(sm["xT1_hi_made"], 1)

            def halve_biases():
                act.wait_ge(small_in["bias"], 32)
                a.mul(hb[:, :, :], hb[:, :, :], 0.5).then_inc(half_bias, 1)
                act.wait_ge(half_bias, 1)

            def gate_tanh(b):
                act.wait_ge(sm["g_done"], b + 1)
                if b >= 1:
                    act.wait_ge(sm["scanned"], b)
                for m in range(KT):
                    last = a.activation(tg[:, m, :], psG[:, m, :], ACT.Tanh, bias=hb[:, 0, m:m + 1], scale=0.5)
                last.then_inc(sm["tg_made"], 1)

            def query_tanh(b):
                act.wait_ge(sm["q_done"], b + 1)
                if b >= 2:
                    act.wait_ge(sm["o_done"], b - 1)
                for m in range(KT):
                    last = a.activation(tq[:, b % 2, m, :], psQ[:, m, :], ACT.Tanh, bias=hb[:, 1, m:m + 1], scale=0.5)
                last.then_inc(sm["tq_made"], 1)

            def turned2(b):
                act.wait_ge(sm["t2_done"], b + 1)
                if b >= 2:
                    act.wait_ge(sm["sim_done"], b - 1)
                a.copy(xT2[:, b % 2], psU).then_inc(sm["xT2_made"], 1)

            def softmax_exp(b):
                act.wait_ge(sm["max_made"], b + 1)
                if b >= 1:
                    act.wait_ge(sm["x3_made"], b)
                for i in range(TB):
                    last = a.activation(ez[:, i, :], z[:, i, :], ACT.Exp, bias=nmax[:, b, i:i + 1],
                                        accum_out=ssum[:, b, i:i + 1])
                last.then_inc(sm["exp_made"], 1)

            def turned3_hi(b):
                act.wait_ge(sm["t3_done"], b + 1)
                if b >= 2:
                    act.wait_ge(sm["lgT_done"], b - 1)
                    act.wait_ge(sm["shg_done"], b - 1)
                    act.wait_ge(sm["shu_done"], b - 1)
                a.copy(xT3_hi[:, b % 2], psM).then_inc(sm["xT3_hi_made"], 1)

            def router_copy(b):
                act.wait_ge(sm["lgT_done"], b + 1)
                if b >= 1:
                    act.wait_ge(sm["lg_done"], b)
                a.copy(lgT[:, :], ps_lgT).then_inc(sm["lgT_copied"], 1)

            def score_tanh(b):
                act.wait_ge(sm["mx_made"], b + 1)
                a.activation(sct[:, b, :], mx[:, b, :], ACT.Tanh, scale=0.5).then_inc(sm["sct_made"], 1)

            def shared_tanh(b):
                act.wait_ge(sm["shg_done"], b + 1)
                if b >= 2:
                    act.wait_ge(sm["sd_done"], b - 1)
                a.activation(hs[:, b % 2], psG, ACT.Tanh, scale=0.5).then_inc(sm["th_made"], 1)

            steps = {"norm1": norm1, "norm2": norm2, "norm3": norm3, "weight_hi": weight_hi, "turned_wk": turned_wk, "turned_ctx": turned_ctx, "kv_bias": kv_bias,
                     "gram_copy": gram_copy, "turned1_hi": turned1_hi, "gate_tanh": gate_tanh,
                     "query_tanh": query_tanh, "turned2": turned2, "softmax_exp": softmax_exp,
                     "turned3_hi": turned3_hi, "router_copy": router_copy, "score_tanh": score_tanh,
                     "shared_tanh": shared_tanh}
            for name, n in steps_of(ACT_ORDER):
                if (name, n) == ("turned1_hi", 0):
                    halve_biases()
                steps[name](n)

            def rows_hi(s, r, reused):
                act.wait_ge(tx_done, s + 1)
                if reused:
                    act.wait_ge(gu_done, s - 1)
                a.copy(xgT_hi[:, r], psX[r][:, :, 0:P]).then_inc(xg_hi_made, 1)

            def tile_tanh(s, r, reused):
                act.wait_ge(gu_done, s + 1)
                if reused:
                    act.wait_ge(th_done, s - 1)
                a.activation(rh[:, r, :], psGU[r][:, 0:D], ACT.Tanh, scale=0.5).then_inc(rth_made, 1)

            def hidden_hi(s, r, reused):
                act.wait_ge(th_done, s + 1)
                if reused:
                    act.wait_ge(down_done, s - 1)
                a.copy(hT_hi[:, r], psH[r][:, :, 0:P]).then_inc(hT_hi_made, 1)

            act.wait_ge(pad_made, 1)
            act.wait_ge(counts_made, 1)
            pad_regions(act, mybir.EngineType.Activation, E // 2, E)
            rows_hi(0, 0, False)
            rows_hi(1, 1, False)
            tile_tanh(0, 0, False)
            rows_hi(2, 0, True)
            for s in range(PEEL):
                tile_tanh(s + 1, (s + 1) % 2, s + 1 >= 2)
                hidden_hi(s, s % 2, s >= 2)
                rows_hi(s + 3, (s + 1) % 2, True)
            with act.Fori(0, LOOPS) as i:
                for j in range(2):
                    s = i * 2 + (PEEL + j)
                    r = (PEEL + j) % 2
                    tile_tanh(s + 1, 1 - r, True)
                    hidden_hi(s, r, True)
                    rows_hi(s + 3, 1 - r, True)
            for s in range(REST, NS):
                if s + 1 < NS:
                    tile_tanh(s + 1, (s + 1) % 2, True)
                hidden_hi(s, s % 2, True)
                if s + 3 < NS:
                    rows_hi(s + 3, (s + 1) % 2, True)

        @block.vector
        def _(dve):
            v = nc.vector
            v.memset(decay[:, :], DECAY).then_inc(dve_consts, 1)
            v.memset(ones[:, :], 1.0)
            v.memset(one_e[:, :], 1.0)
            v.memset(pad[:, :], 0.0).then_inc(dve_consts, 1)
            dve.wait_ge(dve_consts, 2)
            v.memset(pad[:, D:D + 1].bitcast(U32), NOWHERE).then_inc(pad_made, 1)

            def statistics(kind, b, tile):
                for i in range(TB):
                    last = v.bn_stats(bn[:, kind, b, i, :], tile(i))
                last.then_inc(bn_raw[kind], 1)
                dve.wait_ge(bn_raw[kind], b + 1)
                for i in range(TB):
                    last = v.bn_aggr(mv[:, kind, b, i, :], bn[:, kind, b, i, :])
                last.then_inc(stats[kind], 1)

            def stats1(b):
                dve.wait_ge(x_in[b], 16)
                statistics(LN1, b, lambda i: res[:, b * TB + i, :])

            def norm1(b):
                dve.wait_ge(rstd_made[LN1], b + 1)
                for i in range(TB):
                    last = v.tensor_scalar(xn1[:, b % 2, i, :], res[:, b * TB + i, :], mv[:, LN1, b, i, 0:1],
                                           rstd[:, LN1, b, i:i + 1], ALU.subtract, ALU.mult)
                last.then_inc(sm["xn1_made"], 1)

            def weight_lo(n):
                dve.wait_ge(unit_hi, n + 1)
                v.tensor_tensor(units[n][2], stage[:, n % RING], f32(units[n][1]), ALU.subtract).then_inc(proj_lo, 1)

            def turned1_lo(b):
                dve.wait_ge(sm["xT1_hi_made"], b + 1)
                v.tensor_tensor(xT1_lo[:, b % 2], psT, f32(xT1_hi[:, b % 2]), ALU.subtract).then_inc(sm["xT1_lo_made"], 1)

            def turned3_lo(b):
                dve.wait_ge(sm["xT3_hi_made"], b + 1)
                v.tensor_tensor(xT3_lo[:, b % 2], psM, f32(xT3_hi[:, b % 2]), ALU.subtract).then_inc(sm["xT3_lo_made"], 1)

            def memory(b):
                q = tq[:, b % 2]
                dve.wait_ge(sm["tg_made"], b + 1)
                dve.wait_ge(sm["v_done"], b + 1)
                v.scalar_tensor_tensor(tg[:, :, :], tg[:, :, :], 1.0, psV, ALU.add, ALU.mult).then_inc(sm["stored"], 1)
                dve.wait_ge(sm["stored"], b + 1)
                for m in range(KT):
                    last = v.tensor_tensor_scan(mem[:, m, 0:S], decay[:, :], tg[:, m, :], 0.0, ALU.mult, ALU.add)
                last.then_inc(sm["scanned"], 1)
                dve.wait_ge(sm["scanned"], b + 1)
                dve.wait_ge(sm["tq_made"], b + 1)
                v.scalar_tensor_tensor(q, q, 1.0, mem[:, :, 0:S], ALU.add, ALU.mult).then_inc(sm["loaded"], 1)

            def residual2(b):
                rows_b = res[:, b * TB:(b + 1) * TB, :]
                dve.wait_ge(sm["o_done"], b + 1)
                v.scalar_tensor_tensor(rows_b, psO, MEM_SCALE, rows_b, ALU.mult, ALU.add).then_inc(sm["x2_made"], 1)
                dve.wait_ge(sm["x2_made"], b + 1)
                statistics(LN2, b, lambda i: res[:, b * TB + i, :])

            def sim_stats(b):
                dve.wait_ge(sm["sim_done"], b + 1)
                statistics(SIM, b, lambda i: psS[:, i, :])

            def sim_centre(b):
                if b == 0:
                    dve.wait_ge(small_in["gamma"], 16)
                    dve.wait_ge(small_in["beta"], 16)
                else:
                    dve.wait_ge(sm["exp_made"], b)
                dve.wait_ge(stats[SIM], b + 1)
                for i in range(TB):
                    last = v.scalar_tensor_tensor(z[:, i, :], psS[:, i, :], mv[:, SIM, b, i, 0:1], gam[:, :],
                                                  ALU.subtract, ALU.mult)
                last.then_inc(sm["centred"], 1)

            def sim_scale(b):
                dve.wait_ge(sm["centred"], b + 1)
                dve.wait_ge(rstd_made[SIM], b + 1)
                for i in range(TB):
                    last = v.scalar_tensor_tensor(z[:, i, :], z[:, i, :], rstd[:, SIM, b, i:i + 1], bet[:, :],
                                                  ALU.mult, ALU.add)
                last.then_inc(sm["z_made"], 1)
                dve.wait_ge(sm["z_made"], b + 1)
                v.tensor_reduce(nmax[:, b, :], z[:, :, :], AX.X, ALU.max, negate=True).then_inc(sm["max_made"], 1)

            def residual3(b):
                dve.wait_ge(sm["exp_made"], b + 1)
                v.reciprocal(rsum[:, b, :], ssum[:, b, :]).then_inc(sm["rsum_made"], 1)
                dve.wait_ge(sm["rsum_made"], b + 1)
                for i in range(TB):
                    t = b * TB + i
                    last = v.scalar_tensor_tensor(res[:, t, :], ez[:, i, :], rsum[:, b, i:i + 1], res[:, t, :],
                                                  ALU.mult, ALU.add)
                last.then_inc(sm["x3_made"], 1)
                dve.wait_ge(sm["x3_made"], b + 1)
                statistics(LN3, b, lambda i: res[:, b * TB + i, :])

            def route(b):
                n = b + 1
                dve.wait_ge(sm["lg_done"], n)
                v.tensor_copy(lg[:, :, :], ps_lg).then_inc(sm["lg_copied"], 1)
                dve.wait_ge(sm["lg_copied"], n)
                v.tensor_reduce(mx[:, b, :], lg[:, :, :], AX.X, ALU.max).then_inc(sm["mx_made"], 1)
                dve.wait_ge(sm["mx_made"], n)
                v.tensor_tensor(cand[:, :, :], lg[:, :, :], mx[:, b, :].unsqueeze(2).to_broadcast([P, TB, E]), ALU.is_equal).then_inc(sm["eq_made"], 1)
                dve.wait_ge(sm["eq_made"], n)
                dve.wait_ge(consts_made, 1)
                v.tensor_tensor(cand[:, :, :], cand[:, :, :], io_e8[:, :, :], ALU.mult).then_inc(sm["cand_made"], 1)
                dve.wait_ge(sm["cand_made"], n)
                v.tensor_reduce(idx[:, :], cand[:, :, :], AX.X, ALU.min).then_inc(sm["idx_made"], 1)
                dve.wait_ge(sm["idx_made"], n)
                v.tensor_tensor(onehot[:, b * TB:(b + 1) * TB, :], io_e8[:, :, :],
                                idx[:, :].unsqueeze(2).to_broadcast([P, TB, E]), ALU.is_equal).then_inc(sm["onehot_made"], 1)

            def destination(b):
                n = b + 1
                tiles = slice(b * TB, (b + 1) * TB)
                dve.wait_ge(sm["rank_done"], n)
                if b == B - 1:
                    v.tensor_copy(cnt[:, :], ps_count[0:1, :]).then_inc(counts_made, 1)
                v.tensor_tensor(row_e[:, :, :], ps_rank, io_reg[:, :, :], ALU.add).then_inc(sm["row_made"], 1)
                dve.wait_ge(sm["row_made"], n)
                v.tensor_tensor(row_e[:, :, :], row_e[:, :, :], onehot[:, tiles, :], ALU.mult).then_inc(sm["row_picked"], 1)
                dve.wait_ge(sm["row_picked"], n)
                v.tensor_reduce(dest_f[:, tiles], row_e[:, :, :], AX.X, ALU.add).then_inc(sm["dest_summed"], 1)
                dve.wait_ge(sm["dest_summed"], n)
                v.tensor_copy(dest[:, tiles], dest_f[:, tiles]).then_inc(sm["dest_made"], 1)

            def slot_table(_):
                step = [0]

                def link(ins):
                    step[0] += 1
                    ins.then_inc(table_step, 1)
                    dve.wait_ge(table_step, step[0])

                link(v.tensor_tensor(cmp_k[:, :, :], io_k[0:1, :, :], ps_count[0:1, :].unsqueeze(2).to_broadcast([1, E, NT]), ALU.is_lt))
                link(v.tensor_reduce(ntile[:, :], cmp_k[:, :, :], AX.X, ALU.add))
                link(v.tensor_tensor_scan(incl[:, :], one_e[:, :], ntile[:, :], 0.0, ALU.mult, ALU.add))
                link(v.tensor_scalar(tile_s[:, :], io_s[:, :], incl[:, E - 1:E], None, ALU.min))
                link(v.tensor_tensor(cmp_s[:, :, :], tile_s[:, :].unsqueeze(2).to_broadcast([1, NS, E]),
                                     incl[:, :].unsqueeze(1).to_broadcast([1, NS, E]), ALU.is_ge))
                link(v.tensor_reduce(te_f[:, :], cmp_s[:, :, :], AX.X, ALU.add))
                link(v.tensor_tensor(cmp_s[:, :, :], cmp_s[:, :, :], ntile[:, :].unsqueeze(1).to_broadcast([1, NS, E]), ALU.mult))
                link(v.tensor_reduce(before[:, :], cmp_s[:, :, :], AX.X, ALU.add))
                link(v.tensor_tensor(tr_f[:, :], tile_s[:, :], before[:, :], ALU.subtract))
                link(v.tensor_scalar(tr_f[:, :], tr_f[:, :], float(P), None, ALU.mult))
                v.tensor_scalar(te[:, :], te_f[:, :], E - 1.0, None, ALU.min)
                v.scalar_tensor_tensor(tr[:, :], te_f[:, :], float(REGION), tr_f[:, :], ALU.mult, ALU.add).then_inc(table_made, 1)

            def shared_hidden(b):
                h = hs[:, b % 2]
                dve.wait_ge(sm["th_made"], b + 1)
                v.scalar_tensor_tensor(h, h, 1.0, psG, ALU.add, ALU.mult).then_inc(sm["ht_made"], 1)
                dve.wait_ge(sm["ht_made"], b + 1)
                dve.wait_ge(sm["shu_done"], b + 1)
                v.tensor_tensor(h, h, psQ, ALU.mult).then_inc(sm["h_made"], 1)

            def shared_add(b):
                rows_b = res[:, b * TB:(b + 1) * TB, :]
                dve.wait_ge(sm["sd_done"], b + 1)
                v.scalar_tensor_tensor(rows_b, psV, 0.5, rows_b, ALU.mult, ALU.add).then_inc(sm["base_made"], 1)

            def split_router():
                dve.wait_ge(small_in["rw"], 16)
                v.tensor_copy(rw_hi[:, :, :], rw[:, :, :]).then_inc(rw_split, 1)
                dve.wait_ge(rw_split, 1)
                v.tensor_tensor(rw_lo[:, :, :], rw[:, :, :], f32(rw_hi[:, :, :]), ALU.subtract).then_inc(rw_split, 1)

            steps = {"stats1": stats1, "norm1": norm1, "weight_lo": weight_lo, "turned1_lo": turned1_lo,
                     "memory": memory, "residual2": residual2, "sim_stats": sim_stats,
                     "sim_centre": sim_centre, "sim_scale": sim_scale, "residual3": residual3,
                     "turned3_lo": turned3_lo, "route": route, "destination": destination, "slot_table": slot_table,
                     "shared_hidden": shared_hidden, "shared_add": shared_add}
            for name, n in steps_of(DVE_ORDER):
                steps[name](n)
                if (name, n) == ("memory", 0):
                    split_router()

            def hidden(s, r):
                dve.wait_ge(rth_made, s + 1)
                v.scalar_tensor_tensor(rh[:, r, :], rh[:, r, :], 1.0, psGU[r][:, 0:D], ALU.add, ALU.mult).then_inc(rt_made, 1)
                dve.wait_ge(rt_made, s + 1)
                v.tensor_tensor(rh[:, r, :], rh[:, r, :], psGU[r][:, D:2 * D], ALU.mult).then_inc(rh_made, 1)

            def rows_lo(s, r):
                dve.wait_ge(xg_hi_made, s + 1)
                v.tensor_tensor(xgT_lo[:, r], psX[r][:, :, 0:P], f32(xgT_hi[:, r]), ALU.subtract).then_inc(xg_lo_made, 1)
                v.tensor_copy(tid[:, bass.ds(s, 1)], xg[:, r, D:D + 1].bitcast(U32)).then_inc(tid_made, 1)

            def hidden_lo(s, r):
                dve.wait_ge(hT_hi_made, s + 1)
                v.tensor_tensor(hT_lo[:, r], psH[r][:, :, 0:P], f32(hT_hi[:, r]), ALU.subtract).then_inc(hT_lo_made, 1)

            def result(s, r, n):
                dve.wait_ge(down_done, s + 1)
                dve.wait_ge(rb_in[r], (n + 1) * 16)
                dve.wait_ge(written[r], n * 16)
                v.scalar_tensor_tensor(ry[:, r, :], psY[r][:, 0, :], 0.5, rb[:, r, :], ALU.mult, ALU.add).then_inc(y_made, 1)

            rows_lo(0, 0)
            rows_lo(1, 1)
            hidden(0, 0)
            rows_lo(2, 0)
            for s in range(PEEL):
                hidden(s + 1, (s + 1) % 2)
                hidden_lo(s, s % 2)
                if s >= 1:
                    result(s - 1, (s - 1) % 2, (s - 1) // 2)
                rows_lo(s + 3, (s + 1) % 2)
            with dve.Fori(0, LOOPS) as i:
                for j in range(2):
                    s = i * 2 + (PEEL + j)
                    r = (PEEL + j) % 2
                    hidden(s + 1, 1 - r)
                    hidden_lo(s, r)
                    result(s - 1, 1 - r, i + (PEEL + j - 1) // 2)
                    rows_lo(s + 3, 1 - r)
            for s in range(REST, NS + 1):
                if s + 1 < NS:
                    hidden(s + 1, (s + 1) % 2)
                if s < NS:
                    hidden_lo(s, s % 2)
                result(s - 1, (s - 1) % 2, (s - 1) // 2)
                if s + 3 < NS:
                    rows_lo(s + 3, (s + 1) % 2)

        @block.tensor
        def _(pe):
            T = nc.tensor

            def product(out_ap, pairs):
                terms = [(a, c) for a, _, c, _ in pairs] + [(b, c) for _, b, c, _ in pairs] + [(a, d) for a, _, _, d in pairs]
                for i, (l, r) in enumerate(terms):
                    last = T.matmul(out_ap, l, r, start=(i == 0), stop=(i == len(terms) - 1))
                return last

            def turn(ps, rows_of, done):
                for i in range(TB):
                    for k in range(KT):
                        last = T.transpose(ps[:, k, i * P:(i + 1) * P], rows_of[:, i, k * P:(k + 1) * P], ident[:, :])
                last.then_inc(sm[done], 1)

            def turn1(b):
                if b == 0:
                    pe.wait_ge(ident_made, 1)
                pe.wait_ge(sm["xn1_made"], b + 1)
                if b >= 1:
                    pe.wait_ge(sm["xT1_lo_made"], b)
                turn(psT, xn1[:, b % 2], "t1_done")

            def turn2(b):
                pe.wait_ge(sm["xn2_made"], b + 1)
                if b == 0:
                    pe.wait_ge(kvT_made[0], 1)
                else:
                    pe.wait_ge(sm["xT2_made"], b)
                turn(psU, xn2, "t2_done")

            def turn3(b):
                pe.wait_ge(sm["xn3_made"], b + 1)
                if b == 0:
                    pe.wait_ge(gram_made, B)
                else:
                    pe.wait_ge(sm["lg_copied"], b)
                turn(psM, xn3, "t3_done")

            def project(b, w, ps, done, read):
                pe.wait_ge(proj_lo, w + 1)
                pe.wait_ge(sm["xT1_hi_made"], b + 1)
                pe.wait_ge(sm["xT1_lo_made"], b + 1)
                if b >= 1:
                    pe.wait_ge(sm[read], b)
                for m in range(KT):
                    last = product(ps[:, m, :], [(gqv_hi[:, w, k, m * P:(m + 1) * P], gqv_lo[:, w, k, m * P:(m + 1) * P],
                                                  xT1_hi[:, b % 2, k, :], xT1_lo[:, b % 2, k, :]) for k in range(KT)])
                last.then_inc(sm[done], 1)

            def turn_wk(_):
                pe.wait_ge(small_in["wk"], 16)
                pe.wait_ge(ident_made, 1)
                T.transpose(bM[0:C, 0:C], wk_nat[:, :], ident[0:C, 0:C]).then_inc(wk_t, 1)

            def turn_ctx(h):
                pe.wait_ge(small_in["ctx"], 16)
                pe.wait_ge(ident_made, 1)
                for t in range(NT // 2):
                    last = T.transpose((bO, bS)[h][0:C, t * P:(t + 1) * P], ctx_nat[:, h * (NT // 2) + t, :], ident[:, :])
                last.then_inc(ctx_t[h], 1)

            def kv(h):
                pe.wait_ge(ctxT_made[h], 1)
                pe.wait_ge(wkT_made, 1)
                for i in range(2):
                    last = T.matmul((psU, psM)[h][0:C, i, :], wkT[:, :], ctxT(2 * h + i), start=True, stop=True)
                last.then_inc(kv_done[h], 1)

            def gram_product(b):
                pe.wait_ge(kvT_made[b // 2], 1)
                if b == 0:
                    pe.wait_ge(kvT_made[1], 1)
                else:
                    pe.wait_ge(gram_made, b)
                for m in range(KT):
                    last = T.matmul(psM[:, m, :], kvT(b)[:, m * P:(m + 1) * P], kvT(b), start=True, stop=True)
                last.then_inc(gram_done, 1)

            def recall(b):
                pe.wait_ge(small_in["wo"], 16)
                pe.wait_ge(sm["loaded"], b + 1)
                if b == 0:
                    pe.wait_ge(ctxT_made[0], 1)
                else:
                    pe.wait_ge(sm["x2_made"], b)
                for i in range(TB):
                    for m in range(KT):
                        last = T.matmul(psO[:, i, :], tq[:, b % 2, m, i * P:(i + 1) * P], wo[:, m, :],
                                        start=(m == 0), stop=(m == KT - 1))
                last.then_inc(sm["o_done"], 1)

            def similarity(b):
                pe.wait_ge(gram_made, b + 1)
                pe.wait_ge(sm["xT2_made"], b + 1)
                if b == 0:
                    pe.wait_ge(ctxT_made[1], 1)
                else:
                    pe.wait_ge(sm["centred"], b)
                for i in range(TB):
                    for m in range(KT):
                        last = T.matmul(psS[:, i, :], xT2[:, b % 2, m, i * P:(i + 1) * P], gram[:, b, m, :],
                                        start=(m == 0), stop=(m == KT - 1))
                last.then_inc(sm["sim_done"], 1)

            def router(b):
                pe.wait_ge(rw_split, 2)
                pe.wait_ge(sm["xT3_hi_made"], b + 1)
                pe.wait_ge(sm["xT3_lo_made"], b + 1)
                product(ps_lgT, [(rw_hi[:, k, :], rw_lo[:, k, :], xT3_hi[:, b % 2, k, :], xT3_lo[:, b % 2, k, :])
                                 for k in range(KT)]).then_inc(sm["lgT_done"], 1)

            def router_turn(b):
                pe.wait_ge(sm["lgT_copied"], b + 1)
                for i in range(TB):
                    last = T.transpose(ps_lg[:, i, :], lgT[:, i * P:(i + 1) * P], ident[0:E, 0:E])
                last.then_inc(sm["lg_done"], 1)

            def rank(b):
                pe.wait_ge(consts_made, 1)
                pe.wait_ge(dve_consts, 2)
                pe.wait_ge(sm["onehot_made"], b + 1)
                if b == 0:
                    pe.wait_ge(sm["xT1_lo_made"], B)
                else:
                    pe.wait_ge(sm["row_made"], b)
                first = b * TB
                T.matmul(ps_rank, below[:, :], onehot[:, first:first + TB, :], start=True, stop=False)
                for t in range(first):
                    T.matmul(ps_rank, ones[:, :], onehot[:, t, :].unsqueeze(1).to_broadcast([P, TB, E]), start=False, stop=False)
                for i in range(1, TB):
                    for t in range(first, first + i):
                        last = T.matmul(ps_rank[:, i, :], ones[:, :], onehot[:, t, :], start=False, stop=True)
                if b == B - 1:
                    for t in range(NT):
                        last = T.matmul(ps_count, ones[:, :], onehot[:, t, :], start=(t == 0), stop=(t == NT - 1))
                last.then_inc(sm["rank_done"], 1)

            def shared(b, w, ps, done, read):
                pe.wait_ge(unit_lo, w + 1)
                pe.wait_ge(sm["xT3_hi_made"], b + 1)
                pe.wait_ge(sm["xT3_lo_made"], b + 1)
                pe.wait_ge(sm[read], B)
                if b >= 1:
                    pe.wait_ge(sm["h_made"], b)
                for m in range(KT):
                    last = product(ps[:, m, :], [(shw_hi[:, w, k, m * P:(m + 1) * P], shw_lo[:, w, k, m * P:(m + 1) * P],
                                                  xT3_hi[:, b % 2, k, :], xT3_lo[:, b % 2, k, :]) for k in range(KT)])
                last.then_inc(sm[done], 1)

            def shared_down(b):
                pe.wait_ge(small_in["shd"], 16)
                pe.wait_ge(sm["h_made"], b + 1)
                pe.wait_ge(sm["stored"], B)
                if b >= 1:
                    pe.wait_ge(sm["base_made"], b)
                for i in range(TB):
                    for k in range(KT):
                        last = T.matmul(psV[:, i, :], hs[:, b % 2, k, i * P:(i + 1) * P], shd[:, k, :],
                                        start=(k == 0), stop=(k == KT - 1))
                last.then_inc(sm["sd_done"], 1)

            steps = {"turn1": turn1, "turn2": turn2, "turn3": turn3, "turn_wk": turn_wk, "turn_ctx": turn_ctx,
                     "kv": kv, "gram": gram_product, "recall": recall, "similarity": similarity,
                     "gate": lambda b: project(b, 0, psG, "g_done", "tg_made"),
                     "query": lambda b: project(b, 1, psQ, "q_done", "tq_made"),
                     "value": lambda b: project(b, 2, psV, "v_done", "stored"),
                     "router": router, "router_turn": router_turn, "rank": rank,
                     "shared_gate": lambda b: shared(b, 0, psG, "shg_done", "tg_made"),
                     "shared_up": lambda b: shared(b, 1, psQ, "shu_done", "tq_made"),
                     "shared_down": shared_down}
            for name, n in steps_of(PE_ORDER):
                steps[name](n)

            def rows_turn(s, r, loads, reused):
                pe.wait_ge(xg_in[r], loads * 16)
                if reused:
                    pe.wait_ge(xg_lo_made, s - 1)
                for k in range(KT):
                    last = T.transpose(psX[r][:, k, 0:P], xg[:, r, k * P:(k + 1) * P], ident[:, :])
                last.then_inc(tx_done, 1)

            def experts(first, n):
                _, values = nc.values_load_multi_w_load_instructions(
                    te[0:1, bass.ds(first, n)], engines=[mybir.EngineType.PE], min_val=0, max_val=E - 1,
                    skip_runtime_bounds_check_because="slot_table counts experts up from 0 and clamps to E - 1")
                return values

            def gate_up(s, r, e, reused):
                pe.wait_ge(xg_lo_made, s + 1)
                if reused:
                    pe.wait_ge(rh_made, s - 1)
                product(psGU[r][:, :], [(xgT_hi[:, r, k, :], xgT_lo[:, r, k, :], gu_hi[:, e, k, :], gu_lo[:, e, k, :])
                                        for k in range(KT)]).then_inc(gu_done, 1)

            def hidden_turn(s, r, reused):
                pe.wait_ge(rh_made, s + 1)
                if reused:
                    pe.wait_ge(hT_lo_made, s - 1)
                for k in range(KT):
                    last = T.transpose(psH[r][:, k, 0:P], rh[:, r, k * P:(k + 1) * P], ident[:, :])
                last.then_inc(th_done, 1)

            def down(s, r, e, reused):
                pe.wait_ge(hT_lo_made, s + 1)
                if reused:
                    pe.wait_ge(y_made, s - 1)
                product(psY[r][:, 0, :], [(hT_hi[:, r, k, :], hT_lo[:, r, k, :], dn_hi[:, e, k, :], dn_lo[:, e, k, :])
                                          for k in range(KT)]).then_inc(down_done, 1)

            pe.wait_ge(table_made, 1)
            pe.wait_ge(unit_lo, len(units) - PROJ)
            rows_turn(0, 0, 1, False)
            rows_turn(1, 1, 1, False)
            pe.wait_ge(sm["h_made"], B)
            e = experts(0, PEEL + 1)
            gate_up(0, 0, e[0], False)
            rows_turn(2, 0, 2, True)
            pe.wait_ge(sm["base_made"], B)
            for s in range(PEEL):
                gate_up(s + 1, (s + 1) % 2, e[s + 1], s + 1 >= 2)
                hidden_turn(s, s % 2, s >= 2)
                if s >= 1:
                    down(s - 1, (s - 1) % 2, e[s - 1], False)
                rows_turn(s + 3, (s + 1) % 2, (s + 3) // 2 + 1, True)
            with pe.Fori(0, LOOPS) as i:
                e = experts(i * 2 + (PEEL - 1), 4)
                for j in range(2):
                    s = i * 2 + (PEEL + j)
                    r = (PEEL + j) % 2
                    gate_up(s + 1, 1 - r, e[j + 2], True)
                    hidden_turn(s, r, True)
                    down(s - 1, 1 - r, e[j], True)
                    rows_turn(s + 3, 1 - r, i + ((PEEL + j + 3) // 2 + 1), True)
            e = experts(REST - 1, NS - REST + 1)
            for s in range(REST, NS + 1):
                if s + 1 < NS:
                    gate_up(s + 1, (s + 1) % 2, e[s + 1 - (REST - 1)], True)
                if s < NS:
                    hidden_turn(s, s % 2, True)
                down(s - 1, (s - 1) % 2, e[s - REST], True)
                if s + 3 < NS:
                    rows_turn(s + 3, (s + 1) % 2, (s + 3) // 2 + 1, True)


_INS = ["x", "ctx_512", "L0_attn_Wv", "L0_attn_Wg", "L0_attn_bg", "L0_attn_Wq", "L0_attn_bq", "L0_attn_Wo",
        "L0_xattn_W_k", "L0_xattn_b_k", "L0_xattn_ln_gamma", "L0_xattn_ln_beta", "L0_ffn_router_w",
        "L0_ffn_gate_w", "L0_ffn_up_w", "L0_ffn_down_w", "L0_ffn_shared_gate_w", "L0_ffn_shared_up_w",
        "L0_ffn_shared_down_w"]


def kernel(**inputs):
    import numpy as _np
    import concourse.bacc as _bacc
    from concourse import mybir as _mybir
    from concourse.bass_utils import run_bass_kernel_spmd as _run

    nc = _bacc.Bacc("TRN2", target_bir_lowering=False, num_devices=1)
    arrays, args = {}, []
    for name in _INS:
        a = _np.ascontiguousarray(inputs[name])
        arrays[f"in_{name}_dram"] = a
        args.append(nc.dram_tensor(f"in_{name}_dram", a.shape, _mybir.dt.from_np(a.dtype), kind="ExternalInput").ap())
    shape = inputs["x"].shape
    args.append(nc.dram_tensor("out_0_dram", shape, _mybir.dt.float32, kind="ExternalOutput").ap())
    decoder_kernel(nc, *args)
    r = _run(nc, [arrays], core_ids=[0])
    return r.results[0]["out_0_dram"]
```

```python
from contextlib import ExitStack

import concourse.bass as bass
from concourse import mybir
from concourse.alu_op_type import AluOpType as ALU

ACT = mybir.ActivationFunctionType
AX = mybir.AxisListType
F32 = mybir.dt.float32
F32R = mybir.dt.float32r
BF16 = mybir.dt.bfloat16
U32 = mybir.dt.uint32
I32 = mybir.dt.int32

P = 128
LN_EPS = 1e-5
SIM_EPS = 1e-6
DECAY = 0.95

PE_ORDER = """
    turn1:0 turn_ctx:0 turn_wk:0 turn_ctx:1 kv:0 gate:0 turn1:1 value:0 query:0 kv:1 gate:1 query:1
    turn1:2 recall:0 value:1 turn_kv:0 gate:2 query:2 value:2 turn2:0 recall:1 context_mix:0 turn1:3
    similarity:0 recall:2 turn2:1 gate:3 context_mix:1 query:3 similarity:1 value:3 turn2:2
    context_mix:2 turn3:0 similarity:2 recall:3 router:0 shared_up:0 router_turn:0 shared_gate:0
    turn2:3 context_mix:3 similarity:3 turn3:1 rank:0 shared_down:0 router:1 router_turn:1
    shared_up:1 turn3:2 rank:1 shared_gate:1 router:2 router_turn:2 shared_up:2 turn3:3
    shared_gate:2 rank:2 router:3 router_turn:3 shared_down:1 rank:3 shared_gate:3 shared_down:2
    shared_up:3 shared_down:3
""".split()

ACT_ORDER = """
    weight_hi:0 weight_hi:1 weight_hi:2 turned1_hi:0 turned_ctx:0 turned_wk:0 turned_ctx:1 norm1:1
    kv_bias:0 gate_tanh:0 turned1_hi:1 weight_hi:3 weight_hi:4 weight_hi:5 weight_hi:6 query_tanh:0
    kv_bias:1 norm1:2 weight_hi:7 turned1_hi:2 gate_tanh:1 weight_hi:8 weight_hi:9 query_tanh:1
    weight_hi:10 turned_kv:0 weight_hi:11 norm2:0 gate_tanh:2 query_tanh:2 weight_hi:12 turned2:0
    norm1:3 weight_hi:13 mixed:0 turned1_hi:3 norm2:1 weight_hi:14 weight_hi:15 turned2:1
    weight_hi:16 softmax_exp:0 mixed:1 weight_hi:17 gate_tanh:3 norm2:2 query_tanh:3 turned2:2
    norm3:0 mixed:2 turned3_hi:0 weight_hi:18 softmax_exp:1 weight_hi:19 weight_hi:20 router_copy:0
    weight_hi:21 weight_hi:22 norm2:3 shared_tanh:0 weight_hi:23 turned2:3 softmax_exp:2
    weight_hi:24 mixed:3 score_tanh:0 norm3:1 weight_hi:25 weight_hi:26 turned3_hi:1 norm3:2
    router_copy:1 softmax_exp:3 score_tanh:1 turned3_hi:2 shared_tanh:1 weight_hi:27 router_copy:2
    norm3:3 score_tanh:2 turned3_hi:3 shared_tanh:2 router_copy:3 weight_hi:28 score_tanh:3
    shared_tanh:3
""".split()

DVE_ORDER = """
    stats1:0 weight_lo:0 norm1:0 weight_lo:1 stats1:1 weight_lo:2 turned1_lo:0 stats1:2 stats1:3
    turned1_lo:1 memory:0 turned1_lo:2 residual2:0 memory:1 memory:2 residual2:1 turned1_lo:3
    sim_stats:0 sim_centre:0 sim_scale:0 residual2:2 residual3:0 sim_stats:1 sim_centre:1 memory:3
    sim_scale:1 sim_stats:2 turned3_lo:0 residual2:3 sim_centre:2 residual3:1 sim_scale:2
    shared_hidden:0 route:0 residual3:2 sim_stats:3 destination:0 turned3_lo:1 sim_centre:3
    sim_scale:3 route:1 residual3:3 turned3_lo:2 shared_hidden:1 route:2 shared_add:0 destination:1
    turned3_lo:3 destination:2 shared_hidden:2 route:3 shared_add:1 destination:3 slot_table:3
    shared_add:2 shared_hidden:3 shared_add:3
""".split()

POOL_ORDER = """
    rstd1:0 rstd1:1 rstd1:2 rstd1:3 weight_lo:3 weight_lo:4 weight_lo:5 weight_lo:6 weight_lo:7
    weight_lo:8 rstd2:0 weight_lo:9 weight_lo:10 weight_lo:11 weight_lo:12 weight_lo:13 rstd2:1
    sim_rstd:0 weight_lo:14 weight_lo:15 rstd2:2 rstd3:0 sim_rstd:1 weight_lo:16 weight_lo:17
    weight_lo:18 sim_rstd:2 weight_lo:19 rstd2:3 weight_lo:20 weight_lo:21 weight_lo:22 rstd3:1
    scale_rows:0 rstd3:2 sim_rstd:3 scatter:0 weight_lo:23 scale_rows:1 rstd3:3 weight_lo:24
    weight_lo:25 scale_rows:2 scatter:1 scatter:2 scale_rows:3 scatter:3 weight_lo:26 weight_lo:27
    weight_lo:28
""".split()


def steps_of(order):
    for item in order:
        name, _, n = item.partition(":")
        yield name, int(n)


def decoder_kernel(nc, x, ctx_in, Wv, Wg, bg, Wq, bq, Wo, W_k, b_k, gamma, beta,
                   router_w, gate_w, up_w, down_w, sh_gate_w, sh_up_w, sh_down_w, out):
    B, S, D = x.shape
    C = ctx_in.shape[2]
    E = router_w.shape[1]
    KT = D // P
    TB = S // P
    NT = B * TB
    N = B * S
    NS = (N + E * (P - 1)) // P
    REGION = N + P
    W = D + 16
    NOWHERE = 1 << 20
    SIM_SCALE = float(D) ** -0.5
    MEM_SCALE = 0.25 * (1.0 - DECAY)
    PEEL = 3
    LOOPS = (NS - 3 - PEEL) // 2
    REST = PEEL + 2 * LOOPS
    TILE_RING = 2 * KT
    ROUNDS = (NS - 3 - PEEL) // TILE_RING
    RING = 4
    PROJ = 3

    x_sorted = nc.dram_tensor("x_sorted", (E * REGION + P, W), F32, kind="Internal").ap()
    base_rows = nc.dram_tensor("base_rows", (N, D), F32, kind="Internal").ap()
    out_rows = out.rearrange("b s d -> (b s) d")

    with ExitStack() as ctx:
        def sb(name, shape, dt=F32):
            return ctx.enter_context(nc.sbuf_tensor(name, shape, dt))

        def bank(name):
            return ctx.enter_context(nc.psum_tensor(name, [P, 512], F32))

        def sem(name):
            return ctx.enter_context(nc.semaphore(name))

        res = sb("res", [P, NT, D])
        xs = sb("xs", [P, NT, W])
        xn1 = sb("xn1", [P, 2, TB, D])
        xn2 = sb("xn2", [P, TB, D])
        xn3 = sb("xn3", [P, 2, TB, D])
        xT1_hi = sb("xT1_hi", [P, 2, KT, S], F32R)
        xT1_lo = sb("xT1_lo", [P, 2, KT, S], F32R)
        xT2 = sb("xT2", [P, 2, KT, S])
        xT3_hi = sb("xT3_hi", [P, 2, KT, S], F32R)
        xT3_lo = sb("xT3_lo", [P, 2, KT, S], F32R)
        gqv_hi = sb("gqv_hi", [P, PROJ, KT, D], F32R)
        gqv_lo = sb("gqv_lo", [P, PROJ, KT, D], F32R)
        wo = sb("wo", [P, KT, D])
        shw_hi = sb("shw_hi", [P, 2, KT, D], F32R)
        shw_lo = sb("shw_lo", [P, 2, KT, D], F32R)
        shd = sb("shd", [P, KT, D])
        gu_hi = sb("gu_hi", [P, E, KT, 2 * D], F32R)
        gu_lo = sb("gu_lo", [P, E, KT, 2 * D], F32R)
        dn_hi = sb("dn_hi", [P, E, KT, D], F32R)
        dn_lo = sb("dn_lo", [P, E, KT, D], F32R)
        kvT_all = sb("kvT_all", [C, B, S])
        kv_rows = sb("kv_rows", [P, B, KT, C])
        mixT = sb("mixT", [C, 2, S])
        stage = sb("stage", [P, RING, KT, D])
        tg = sb("tg", [P, KT, S])
        tq = sb("tq", [P, 2, KT, S])
        mem = sb("mem", [P, 2, W])
        z = sb("z", [P, TB, S])
        ez = sb("ez", [P, TB, S])
        hs = xn1
        ctx_nat = ez[:, :, :].rearrange("p i (t c) -> p (i t) c", c=C)
        wk_nat = sb("wk_nat", [C, C])
        wkT = sb("wkT", [C, C])
        bk = sb("bk", [C, 1])
        hb = sb("hb", [P, 2, KT])
        gam = sb("gam", [P, S])
        bet = sb("bet", [P, S])
        decay = sb("decay", [P, S])
        pad = sb("pad", [P, W])
        ident = sb("ident", [P, P])
        below = sb("below", [P, P], BF16)
        ones = sb("ones", [P, P], BF16)
        expo = sb("expo", [P, TB])
        rw = sb("rw", [P, KT, E])
        rw_hi = sb("rw_hi", [P, KT, E], F32R)
        rw_lo = sb("rw_lo", [P, KT, E], F32R)
        lgT = sb("lgT", [E, S])
        io_e8 = sb("io_e8", [P, TB, E])
        io_reg = sb("io_reg", [P, TB, E])
        io_k = sb("io_k", [P, E, NT])
        io_s = sb("io_s", [1, NS])
        bn = sb("bn", [P, 4, B, TB, 6])
        mv = sb("mv", [P, 4, B, TB, 2])
        vareps = sb("vareps", [P, 4, B, TB])
        rstd = sb("rstd", [P, 4, B, TB])
        shift = sb("shift", [P, 4, B, TB])
        nmax = sb("nmax", [P, B, TB])
        ssum = sb("ssum", [P, B, TB])
        rsum = sb("rsum", [P, B, TB])
        lg = sb("lg", [P, TB, E])
        mx = sb("mx", [P, B, TB])
        sct = sb("sct", [P, B, TB])
        score = sb("score", [P, B, TB])
        cand = sb("cand", [P, TB, E])
        idx = sb("idx", [P, TB])
        onehot = sb("onehot", [P, NT, E], BF16)
        row_e = sb("row_e", [P, TB, E])
        dest_f = sb("dest_f", [P, NT])
        dest = sb("dest", [P, NT], U32)
        cmp_k = sb("cmp_k", [1, E, NT])
        ntile = sb("ntile", [1, E])
        one_e = sb("one_e", [1, E])
        incl = sb("incl", [1, E])
        tile_s = sb("tile_s", [1, NS])
        cmp_s = sb("cmp_s", [1, NS, E])
        te_f = sb("te_f", [1, NS])
        before = sb("before", [1, NS])
        tr_f = sb("tr_f", [1, NS])
        te = sb("te", [1, NS], I32)
        tr = sb("tr", [1, NS], I32)
        cnt = sb("cnt", [1, E], I32)
        tid = sb("tid", [P, NS], U32)
        xg = xs
        xgT_hi, xgT_lo = xT1_hi[:, :, :, 0:P], xT1_lo[:, :, :, 0:P]
        hT_hi, hT_lo = xT1_hi[:, :, :, P:2 * P], xT1_lo[:, :, :, P:2 * P]
        rh = tg
        rb = tq[:, :, :, :].rearrange("p b k s -> p (b k) s")
        ry = z

        bT, bU, bG, bQ, bV, bO, bS, bM = [bank(n) for n in ("bT", "bU", "bG", "bQ", "bV", "bO", "bS", "bM")]

        def halves(b):
            return b[:, :].rearrange("p (k n) -> p k n", k=2)

        psT, psU, psG, psQ, psV, psO, psS, psM = [halves(b) for b in (bT, bU, bG, bQ, bV, bO, bS, bM)]
        ps_lgT = bM[0:E, 0:S]
        ps_lg = bM[:, S:S + TB * E].rearrange("p (t e) -> p t e", e=E)
        ps_rank = bT[:, 0:TB * E].rearrange("p (t e) -> p t e", e=E)
        ps_count = bT[:, TB * E:TB * E + E]
        ps_kv = bS[:, :].rearrange("p (b k c) -> p b k c", b=B, c=C)
        psX, psH, psGU, psY = [psT, psS], [psU, psM], [bG, bQ], [psV, psO]

        x_in = [sem(f"x_in{b}") for b in range(B)]
        small_in = {n: sem(f"{n}_in") for n in ("wk", "ctx", "bk", "bias", "wo", "gamma", "beta", "rw", "shd")}
        stage_in = [sem(f"stage_in{r}") for r in range(RING)]
        unit_hi, proj_lo, unit_lo = sem("unit_hi"), sem("proj_lo"), sem("unit_lo")
        ident_raw, ident_made, below_raw, consts_made = sem("ident_raw"), sem("ident_made"), sem("below_raw"), sem("consts_made")
        dve_consts, rows_raw, rows_ready, pad_made = sem("dve_consts"), sem("rows_raw"), sem("rows_ready"), sem("pad_made")
        half_bias, rw_split = sem("half_bias"), sem("rw_split")
        KINDS = LN1, LN2, SIM, LN3 = range(4)
        bn_raw, stats, eps_added, rstd_made, negated, shift_made = ([sem(f"{n}{kind}") for kind in KINDS] for n in
                                                           ("bn_raw", "stats", "eps_added", "rstd_made", "negated", "shift_made"))
        names = ("xn1_made", "t1_done", "xT1_hi_made", "xT1_lo_made", "g_done", "q_done", "v_done",
                 "tg_made", "tq_made", "stored", "scanned", "loaded", "o_done",
                 "x2_made", "xn2_made", "t2_done", "xT2_made", "mix_done", "mixT_made", "sim_done", "centred",
                 "z_made", "max_made", "exp_made", "rsum_made", "x3_made", "xn3_made",
                 "t3_done", "xT3_hi_made", "xT3_lo_made", "lgT_done", "lgT_copied", "lg_done", "lg_copied",
                 "mx_made", "sct_made", "score_made", "xs_made", "eq_made", "cand_made", "idx_made", "onehot_made",
                 "rank_done", "row_made", "row_picked", "dest_summed", "dest_made",
                 "shg_done", "shu_done", "th_made", "ht_made", "h_made", "sd_done", "base_made")
        sm = {n: sem(n) for n in names}
        wk_t, wkT_made = sem("wk_t"), sem("wkT_made")
        ctx_t, ctxT_made, kv_done, kvT_made = ([sem(f"{n}{h}") for h in range(2)]
                                               for n in ("ctx_t", "ctxT_made", "kv_done", "kvT_made"))
        kv_rows_done, kv_rows_made = sem("kv_rows_done"), sem("kv_rows_made")
        table_step, counts_made, table_made = sem("table_step"), sem("counts_made"), sem("table_made")
        base_out, padded, scattered = sem("base_out"), sem("padded"), sem("scattered")
        xg_in, rb_in = [sem(f"xg_in{r}") for r in range(TILE_RING)], [sem(f"rb_in{r}") for r in range(TILE_RING)]
        tid_made = sem("tid_made")
        tx_done, xg_hi_made, xg_lo_made = sem("tx_done"), sem("xg_hi_made"), sem("xg_lo_made")
        gu_done, rth_made, rt_made, rh_made = sem("gu_done"), sem("rth_made"), sem("rt_made"), sem("rh_made")
        th_done, hT_hi_made, hT_lo_made = sem("th_done"), sem("hT_hi_made"), sem("hT_lo_made")
        down_done, y_made = sem("down_done"), sem("y_made")
        written = [sem("written0"), sem("written1")]

        def rows(w):
            return w.rearrange("(k p) n -> p k n", p=P)

        units = [(rows(w), gqv_hi[:, i], gqv_lo[:, i]) for i, w in enumerate((Wg, Wq, Wv))]
        units += [(rows(w), shw_hi[:, i], shw_lo[:, i]) for i, w in enumerate((sh_gate_w, sh_up_w))]
        for e in range(E):
            units += [(rows(gate_w[e]), gu_hi[:, e, :, 0:D], gu_lo[:, e, :, 0:D]),
                      (rows(up_w[e]), gu_hi[:, e, :, D:2 * D], gu_lo[:, e, :, D:2 * D]),
                      (rows(down_w[e]), dn_hi[:, e], dn_lo[:, e])]
        SHARED_LO = 2

        def f32(ap):
            return ap.bitcast(F32)

        def ctxT(b):
            return xs[0:C, b, 0:S]

        def kvT(b):
            return kvT_all[:, b, :]

        def pad_regions(queue, engine, first, last):
            _, count = nc.values_load_multi_w_load_instructions(
                cnt[0:1, first:last], engines=[engine], min_val=0, max_val=N,
                skip_runtime_bounds_check_because="a count of tokens is at most all of them")
            for e in range(first, last):
                queue.dma_start(x_sorted[bass.ds(count[e - first] + e * REGION, P), :], pad[:, :]).then_inc(padded, 16)

        block = ctx.enter_context(nc.Block())

        @block.sync
        def _(sp):
            def load_x(b):
                sp.dma_start(res[:, b * TB:(b + 1) * TB, :], x[b].rearrange("(t p) d -> p t d", p=P)).then_inc(x_in[b], 16)

            def load_unit(n):
                if n >= RING:
                    old = n - RING
                    sp.wait_ge(unit_hi, old + 1)
                    if old < PROJ:
                        sp.wait_ge(proj_lo, old + 1)
                    else:
                        sp.wait_ge(unit_lo, old - PROJ + 1)
                sp.dma_start(stage[:, n % RING], units[n][0]).then_inc(stage_in[n % RING], 16)

            def load(name, dst, src, scattered_words=False):
                sp.dma_start(dst, src, allow_slow_non_contiguous=scattered_words).then_inc(small_in[name], 16)

            load_x(0)
            load_unit(0)
            load_unit(1)
            load_unit(2)
            load("ctx", ctx_nat, ctx_in.rearrange("b (t p) c -> p (b t) c", p=P))
            load("wk", wk_nat[:, :], W_k)
            load("bias", hb[:, 0, :], bg.rearrange("(m p) -> p m", p=P), True)
            load("bias", hb[:, 1, :], bq.rearrange("(m p) -> p m", p=P), True)
            load("bk", bk[:, :], b_k.rearrange("(p o) -> p o", o=1))
            load_x(1)
            load("wo", wo[:, :, :], rows(Wo))
            load_x(2)
            load_x(3)
            load("gamma", gam[:, :], gamma.unsqueeze(0).to_broadcast([P, S]))
            load("beta", bet[:, :], beta.unsqueeze(0).to_broadcast([P, S]))
            load("rw", rw[:, :, :], router_w.rearrange("(k p) e -> p k e", p=P))
            for n in range(PROJ, len(units)):
                load_unit(n)
                if n == RING:
                    load("shd", shd[:, :, :], rows(sh_down_w))

            def store_base(b):
                sp.wait_ge(sm["base_made"], b + 1)
                sp.dma_start(base_rows[b * S:(b + 1) * S, :].rearrange("(t p) d -> p t d", p=P),
                             res[:, b * TB:(b + 1) * TB, :]).then_inc(base_out, 16)

            for b in range(B - 2):
                store_base(b)
            sp.wait_ge(pad_made, 1)
            sp.dma_start(x_sorted[E * REGION:E * REGION + P, :], pad[:, :]).then_inc(padded, 16)
            sp.wait_ge(counts_made, 1)
            pad_regions(sp, mybir.EngineType.SP, 0, E // 2)

            def first_rows(s, n):
                _, values = nc.values_load_multi_w_load_instructions(
                    tr[0:1, bass.ds(s, n)], engines=[mybir.EngineType.SP], min_val=0, max_val=E * REGION,
                    skip_runtime_bounds_check_because="slot_table's rows start a tile of a region or the padding behind them")
                return values

            def load_rows(r, row):
                sp.dma_start(xg[:, r, :], x_sorted[bass.ds(row, P), :]).then_inc(xg_in[r], 16)

            sp.wait_ge(table_made, 1)
            row = first_rows(0, TILE_RING)
            sp.wait_ge(padded, 16 * (E + 1))
            sp.wait_ge(scattered, 16 * NT)
            for q in range(TILE_RING):
                load_rows(q, row[q])
            for b in range(B - 2, B):
                store_base(b)
            with sp.Fori(0, NS // TILE_RING - 1) as i:
                row = first_rows(i * TILE_RING + TILE_RING, TILE_RING)
                for q in range(TILE_RING):
                    sp.wait_ge(tx_done, i * TILE_RING + (q + 1))
                    sp.wait_ge(tid_made, i * TILE_RING + (q + 1))
                    load_rows(q, row[q])
            row = first_rows(NS - NS % TILE_RING, NS % TILE_RING)
            for q in range(NS % TILE_RING):
                sp.wait_ge(tx_done, NS - NS % TILE_RING - TILE_RING + q + 1)
                sp.wait_ge(tid_made, NS - NS % TILE_RING - TILE_RING + q + 1)
                load_rows(q, row[q])

        @block.gpsimd
        def _(pool):
            g = nc.gpsimd
            g.memset(ident[:, :], 0.0).then_inc(ident_raw, 1)
            g.memset(expo[:, :], -0.5).then_inc(ident_raw, 1)
            pool.wait_ge(ident_raw, 2)
            g.affine_select(out=ident[:, :], in_=ident[:, :], compare_op=ALU.not_equal, fill=1.0, base=0,
                            pattern=[[-1, P]], channel_multiplier=1).then_inc(ident_made, 1)
            g.memset(below[:, :], 1.0).then_inc(below_raw, 1)
            g.iota(io_e8[:, :, :], [[0, TB], [1, E]], -E, 0, True)
            g.iota(io_reg[:, :, :], [[0, TB], [REGION, E]], 0, 0, True)
            g.iota(io_k[:, :, :], [[0, E], [P, NT]], 0, 0, True)
            g.iota(io_s[:, :], [[1, NS]], 0, 0, True)
            g.memset(xs[:, :, D:W], 0.0).then_inc(rows_raw, 1)
            pool.wait_ge(rows_raw, 1)
            g.iota(xs[:, :, D:D + 1].bitcast(U32), [[P, NT], [1, 1]], 0, 1, True).then_inc(rows_ready, 1)
            pool.wait_ge(below_raw, 1)
            g.affine_select(out=below[:, :], in_=below[:, :], compare_op=ALU.is_gt, fill=0.0, base=0,
                            pattern=[[1, P]], channel_multiplier=-1).then_inc(consts_made, 1)

            def rsqrt(kind, b):
                eps = SIM_EPS / SIM_SCALE ** 2 if kind == SIM else LN_EPS
                pool.wait_ge(stats[kind], b + 1)
                g.tensor_scalar(vareps[:, kind, b, :], mv[:, kind, b, :, 1], eps, None, ALU.add).then_inc(eps_added[kind], 1)
                if kind != SIM and (kind, b) != (LN1, 0):
                    g.tensor_scalar(shift[:, kind, b, :], mv[:, kind, b, :, 0], -1.0, None, ALU.mult).then_inc(negated[kind], 1)
                pool.wait_ge(eps_added[kind], b + 1)
                g.tensor_tensor(rstd[:, kind, b, :], vareps[:, kind, b, :], expo[:, :], ALU.pow).then_inc(rstd_made[kind], 1)
                if kind != SIM and (kind, b) != (LN1, 0):
                    pool.wait_ge(negated[kind], b + 1 if kind != LN1 else b)
                    pool.wait_ge(rstd_made[kind], b + 1)
                    g.tensor_tensor(shift[:, kind, b, :], shift[:, kind, b, :], rstd[:, kind, b, :],
                                    ALU.mult).then_inc(shift_made[kind], 1)

            def scale_rows(b):
                pool.wait_ge(sm["sct_made"], b + 1)
                g.tensor_scalar(score[:, b, :], sct[:, b, :], 0.5, 0.5, ALU.mult, ALU.add).then_inc(sm["score_made"], 1)
                pool.wait_ge(sm["score_made"], b + 1)
                if b == 0:
                    pool.wait_ge(kv_done[0], 1)
                    pool.wait_ge(kv_done[1], 1)
                for i in range(TB):
                    last = g.tensor_scalar(xs[:, b * TB + i, 0:D], xn3[:, b % 2, i, :], score[:, b, i:i + 1], 1.0, ALU.mult, ALU.mult)
                last.then_inc(sm["xs_made"], 1)

            def scatter(b):
                pool.wait_ge(sm["dest_made"], b + 1)
                pool.wait_ge(sm["xs_made"], b + 1)
                pool.wait_ge(rows_ready, 1)
                for t in range(b * TB, (b + 1) * TB):
                    g.indirect_dma_start(x_sorted, bass.IndirectOffsetOnAxis(dest[:, t:t + 1], 0), xs[:, t, :], None,
                                         bounds_check=E * REGION - 1, oob_is_err=False).then_inc(scattered, 16)

            def weight_lo(n):
                pool.wait_ge(unit_hi, n + 1)
                g.tensor_tensor(units[n][2], stage[:, n % RING], f32(units[n][1]), ALU.subtract).then_inc(unit_lo, 1)

            steps = {"rstd1": lambda b: rsqrt(LN1, b),
                     "rstd2": lambda b: rsqrt(LN2, b),
                     "sim_rstd": lambda b: rsqrt(SIM, b),
                     "rstd3": lambda b: rsqrt(LN3, b),
                     "scale_rows": scale_rows, "scatter": scatter, "weight_lo": weight_lo}
            for name, n in steps_of(POOL_ORDER):
                steps[name](n)

            def gather(s):
                pool.wait_ge(tid_made, s + 1)
                if s >= TILE_RING:
                    pool.wait_ge(y_made, s - TILE_RING + 1)
                g.indirect_dma_start(rb[:, s % TILE_RING, :], None, base_rows, bass.IndirectOffsetOnAxis(tid[:, s:s + 1], 0),
                                     bounds_check=N - 1, oob_is_err=False).then_inc(rb_in[s % TILE_RING], 16)

            def write(s):
                pool.wait_ge(y_made, s + 1)
                g.indirect_dma_start(out_rows, bass.IndirectOffsetOnAxis(tid[:, s:s + 1], 0), ry[:, s % 2, :], None,
                                     bounds_check=N - 1, oob_is_err=False).then_inc(written[s % 2], 16)

            pool.wait_ge(base_out, 16 * B)
            for s in range(TILE_RING - 1):
                gather(s)
            for s in range(NS):
                if s + TILE_RING - 1 < NS:
                    gather(s + TILE_RING - 1)
                write(s)
            pool.wait_ge(written[0], 16 * ((NS + 1) // 2))
            pool.wait_ge(written[1], 16 * (NS // 2))

        @block.scalar
        def _(act):
            a = nc.scalar

            def normalise(kind, b, dst, made):
                act.wait_ge(shift_made[kind], b + 1 if kind != LN1 else b)
                for i in range(TB):
                    last = a.activation(dst[:, i, :], res[:, b * TB + i, :], ACT.Identity, bias=shift[:, kind, b, i:i + 1],
                                        scale=rstd[:, kind, b, i:i + 1])
                last.then_inc(sm[made], 1)

            def norm1(b):
                if b == 1:
                    act.wait_ge(sm["xn1_made"], 1)
                if b >= 2:
                    act.wait_ge(sm["t1_done"], b - 1)
                normalise(LN1, b, xn1[:, b % 2], "xn1_made")

            def norm2(b):
                if b >= 1:
                    act.wait_ge(sm["t2_done"], b)
                normalise(LN2, b, xn2, "xn2_made")

            def norm3(b):
                if b >= 2:
                    act.wait_ge(sm["t3_done"], b - 1)
                    act.wait_ge(sm["xs_made"], b - 1)
                normalise(LN3, b, xn3[:, b % 2], "xn3_made")

            def weight_hi(n):
                act.wait_ge(stage_in[n % RING], 16 * (n // RING + 1))
                a.copy(units[n][1], stage[:, n % RING]).then_inc(unit_hi, 1)

            def turned_wk(_):
                act.wait_ge(wk_t, 1)
                a.copy(wkT[:, :], bM[0:C, 0:C]).then_inc(wkT_made, 1)

            def turned_ctx(h):
                act.wait_ge(ctx_t[h], 1)
                if h == 0:
                    act.wait_ge(rows_ready, 1)
                a.copy(xs[0:C, 2 * h:2 * h + 2, 0:S], (psO, psS)[h][0:C]).then_inc(ctxT_made[h], 1)

            def kv_bias(h):
                act.wait_ge(kv_done[h], 1)
                act.wait_ge(small_in["bk"], 16)
                a.activation(kvT_all[:, 2 * h:2 * h + 2, :], (psU, psM)[h][0:C], ACT.Identity,
                             bias=bk[:, :]).then_inc(kvT_made[h], 1)

            def turned_kv(_):
                act.wait_ge(kv_rows_done, 1)
                a.copy(kv_rows[:, :, :, :], ps_kv).then_inc(kv_rows_made, 1)

            def mixed(b):
                act.wait_ge(sm["mix_done"], b + 1)
                if b >= 2:
                    act.wait_ge(sm["sim_done"], b - 1)
                a.copy(mixT[:, b % 2, :], bU[0:C, 0:S]).then_inc(sm["mixT_made"], 1)

            def turned1_hi(b):
                act.wait_ge(sm["t1_done"], b + 1)
                if b >= 2:
                    act.wait_ge(sm["g_done"], b - 1)
                    act.wait_ge(sm["q_done"], b - 1)
                    act.wait_ge(sm["v_done"], b - 1)
                a.copy(xT1_hi[:, b % 2], psT).then_inc(sm["xT1_hi_made"], 1)

            def halve_biases():
                act.wait_ge(small_in["bias"], 32)
                a.mul(hb[:, :, :], hb[:, :, :], 0.5).then_inc(half_bias, 1)
                act.wait_ge(half_bias, 1)

            def gate_tanh(b):
                act.wait_ge(sm["g_done"], b + 1)
                if b >= 1:
                    act.wait_ge(sm["scanned"], b * KT)
                for m in range(KT):
                    last = a.activation(tg[:, m, :], psG[:, m, :], ACT.Tanh, bias=hb[:, 0, m:m + 1], scale=0.5)
                last.then_inc(sm["tg_made"], 1)

            def query_tanh(b):
                act.wait_ge(sm["q_done"], b + 1)
                if b >= 2:
                    act.wait_ge(sm["o_done"], b - 1)
                for m in range(KT):
                    last = a.activation(tq[:, b % 2, m, :], psQ[:, m, :], ACT.Tanh, bias=hb[:, 1, m:m + 1], scale=0.5)
                last.then_inc(sm["tq_made"], 1)

            def turned2(b):
                act.wait_ge(sm["t2_done"], b + 1)
                if b >= 2:
                    act.wait_ge(sm["mix_done"], b - 1)
                a.copy(xT2[:, b % 2], psU).then_inc(sm["xT2_made"], 1)

            def softmax_exp(b):
                act.wait_ge(sm["max_made"], b + 1)
                if b >= 1:
                    act.wait_ge(sm["x3_made"], b * TB)
                for i in range(TB):
                    last = a.activation(ez[:, i, :], z[:, i, :], ACT.Exp, bias=nmax[:, b, i:i + 1],
                                        accum_out=ssum[:, b, i:i + 1])
                last.then_inc(sm["exp_made"], 1)

            def turned3_hi(b):
                act.wait_ge(sm["t3_done"], b + 1)
                if b >= 2:
                    act.wait_ge(sm["lgT_done"], b - 1)
                    act.wait_ge(sm["shg_done"], b - 1)
                    act.wait_ge(sm["shu_done"], b - 1)
                a.copy(xT3_hi[:, b % 2], psM).then_inc(sm["xT3_hi_made"], 1)

            def router_copy(b):
                act.wait_ge(sm["lgT_done"], b + 1)
                if b >= 1:
                    act.wait_ge(sm["lg_done"], b)
                a.copy(lgT[:, :], ps_lgT).then_inc(sm["lgT_copied"], 1)

            def score_tanh(b):
                act.wait_ge(sm["mx_made"], b + 1)
                a.activation(sct[:, b, :], mx[:, b, :], ACT.Tanh, scale=0.5).then_inc(sm["sct_made"], 1)

            def shared_tanh(b):
                act.wait_ge(sm["shg_done"], b + 1)
                if b >= 2:
                    act.wait_ge(sm["sd_done"], b - 1)
                a.activation(hs[:, b % 2], psG, ACT.Tanh, scale=0.5).then_inc(sm["th_made"], 1)

            steps = {"norm1": norm1, "norm2": norm2, "norm3": norm3, "weight_hi": weight_hi, "turned_wk": turned_wk, "turned_ctx": turned_ctx, "kv_bias": kv_bias,
                     "turned_kv": turned_kv, "mixed": mixed, "turned1_hi": turned1_hi, "gate_tanh": gate_tanh,
                     "query_tanh": query_tanh, "turned2": turned2, "softmax_exp": softmax_exp,
                     "turned3_hi": turned3_hi, "router_copy": router_copy, "score_tanh": score_tanh,
                     "shared_tanh": shared_tanh}
            halved = False
            for name, n in steps_of(ACT_ORDER):
                if name in ("gate_tanh", "query_tanh") and not halved:
                    halve_biases()
                    halved = True
                if (name, n) == ("shared_tanh", B - 1):
                    act.wait_ge(pad_made, 1)
                    act.wait_ge(counts_made, 1)
                    pad_regions(act, mybir.EngineType.Activation, E // 2, E)
                steps[name](n)

            def rows_hi(s, r, reused):
                act.wait_ge(tx_done, s + 1)
                if reused:
                    act.wait_ge(gu_done, s - 1)
                a.copy(xgT_hi[:, r], psX[r][:, :, 0:P]).then_inc(xg_hi_made, 1)

            def tile_tanh(s, r, reused):
                act.wait_ge(gu_done, s + 1)
                if reused:
                    act.wait_ge(th_done, s - 1)
                a.activation(rh[:, r, :], psGU[r][:, 0:D], ACT.Tanh, scale=0.5).then_inc(rth_made, 1)

            def hidden_hi(s, r, reused):
                act.wait_ge(th_done, s + 1)
                if reused:
                    act.wait_ge(down_done, s - 1)
                a.copy(hT_hi[:, r], psH[r][:, :, 0:P]).then_inc(hT_hi_made, 1)

            rows_hi(0, 0, False)
            rows_hi(1, 1, False)
            tile_tanh(0, 0, False)
            rows_hi(2, 0, True)
            for s in range(PEEL):
                tile_tanh(s + 1, (s + 1) % 2, s + 1 >= 2)
                hidden_hi(s, s % 2, s >= 2)
                rows_hi(s + 3, (s + 1) % 2, True)
            with act.Fori(0, LOOPS) as i:
                for j in range(2):
                    s = i * 2 + (PEEL + j)
                    r = (PEEL + j) % 2
                    tile_tanh(s + 1, 1 - r, True)
                    hidden_hi(s, r, True)
                    rows_hi(s + 3, 1 - r, True)
            for s in range(REST, NS):
                if s + 1 < NS:
                    tile_tanh(s + 1, (s + 1) % 2, True)
                hidden_hi(s, s % 2, True)
                if s + 3 < NS:
                    rows_hi(s + 3, (s + 1) % 2, True)

        @block.vector
        def _(dve):
            v = nc.vector
            v.memset(decay[:, :], DECAY).then_inc(dve_consts, 1)
            v.memset(ones[:, :], 1.0)
            v.memset(one_e[:, :], 1.0)
            v.memset(pad[:, :], 0.0).then_inc(dve_consts, 1)
            dve.wait_ge(dve_consts, 2)
            v.memset(pad[:, D:D + 1].bitcast(U32), NOWHERE).then_inc(pad_made, 1)

            def statistics(kind, b, tile, updated=None):
                for i in range(TB):
                    if updated:
                        dve.wait_ge(sm[updated], b * TB + i + 1)
                    v.bn_stats(bn[:, kind, b, i, :], tile(i)).then_inc(bn_raw[kind], 1)
                for i in range(TB):
                    dve.wait_ge(bn_raw[kind], b * TB + i + 1)
                    last = v.bn_aggr(mv[:, kind, b, i, :], bn[:, kind, b, i, :])
                last.then_inc(stats[kind], 1)

            def stats1(b):
                dve.wait_ge(x_in[b], 16)
                statistics(LN1, b, lambda i: res[:, b * TB + i, :])

            def norm1(b):
                dve.wait_ge(rstd_made[LN1], b + 1)
                for i in range(TB):
                    last = v.tensor_scalar(xn1[:, b % 2, i, :], res[:, b * TB + i, :], mv[:, LN1, b, i, 0:1],
                                           rstd[:, LN1, b, i:i + 1], ALU.subtract, ALU.mult)
                last.then_inc(sm["xn1_made"], 1)

            def weight_lo(n):
                dve.wait_ge(unit_hi, n + 1)
                v.tensor_tensor(units[n][2], stage[:, n % RING], f32(units[n][1]), ALU.subtract).then_inc(proj_lo, 1)

            def turned1_lo(b):
                dve.wait_ge(sm["xT1_hi_made"], b + 1)
                v.tensor_tensor(xT1_lo[:, b % 2], psT, f32(xT1_hi[:, b % 2]), ALU.subtract).then_inc(sm["xT1_lo_made"], 1)

            def turned3_lo(b):
                dve.wait_ge(sm["xT3_hi_made"], b + 1)
                v.tensor_tensor(xT3_lo[:, b % 2], psM, f32(xT3_hi[:, b % 2]), ALU.subtract).then_inc(sm["xT3_lo_made"], 1)

            def memory(b):
                q = tq[:, b % 2]
                dve.wait_ge(sm["tg_made"], b + 1)
                dve.wait_ge(sm["v_done"], b + 1)
                for m in range(KT):
                    v.scalar_tensor_tensor(tg[:, m, :], tg[:, m, :], 1.0, psV[:, m, :], ALU.add, ALU.mult).then_inc(sm["stored"], 1)
                for m in range(KT):
                    dve.wait_ge(sm["stored"], b * KT + m + 1)
                    v.tensor_tensor_scan(mem[:, m, 0:S], decay[:, :], tg[:, m, :], 0.0, ALU.mult, ALU.add).then_inc(sm["scanned"], 1)
                dve.wait_ge(sm["tq_made"], b + 1)
                for m in range(KT):
                    dve.wait_ge(sm["scanned"], b * KT + m + 1)
                    last = v.scalar_tensor_tensor(q[:, m, :], q[:, m, :], 1.0, mem[:, m, 0:S], ALU.add, ALU.mult)
                last.then_inc(sm["loaded"], 1)

            def residual2(b):
                dve.wait_ge(sm["o_done"], b + 1)
                for i in range(TB):
                    t = b * TB + i
                    v.scalar_tensor_tensor(res[:, t, :], psO[:, i, :], MEM_SCALE, res[:, t, :], ALU.mult, ALU.add).then_inc(sm["x2_made"], 1)
                statistics(LN2, b, lambda i: res[:, b * TB + i, :], "x2_made")

            def sim_stats(b):
                dve.wait_ge(sm["sim_done"], b + 1)
                statistics(SIM, b, lambda i: psS[:, i, :])

            def sim_centre(b):
                if b == 0:
                    dve.wait_ge(small_in["gamma"], 16)
                    dve.wait_ge(small_in["beta"], 16)
                else:
                    dve.wait_ge(sm["exp_made"], b)
                dve.wait_ge(stats[SIM], b + 1)
                for i in range(TB):
                    last = v.scalar_tensor_tensor(z[:, i, :], psS[:, i, :], mv[:, SIM, b, i, 0:1], gam[:, :],
                                                  ALU.subtract, ALU.mult)
                last.then_inc(sm["centred"], 1)

            def sim_scale(b):
                dve.wait_ge(sm["centred"], b + 1)
                dve.wait_ge(rstd_made[SIM], b + 1)
                for i in range(TB):
                    last = v.scalar_tensor_tensor(z[:, i, :], z[:, i, :], rstd[:, SIM, b, i:i + 1], bet[:, :],
                                                  ALU.mult, ALU.add)
                last.then_inc(sm["z_made"], 1)
                dve.wait_ge(sm["z_made"], b + 1)
                v.tensor_reduce(nmax[:, b, :], z[:, :, :], AX.X, ALU.max, negate=True).then_inc(sm["max_made"], 1)

            def residual3(b):
                dve.wait_ge(sm["exp_made"], b + 1)
                v.reciprocal(rsum[:, b, :], ssum[:, b, :]).then_inc(sm["rsum_made"], 1)
                dve.wait_ge(sm["rsum_made"], b + 1)
                for i in range(TB):
                    t = b * TB + i
                    v.scalar_tensor_tensor(res[:, t, :], ez[:, i, :], rsum[:, b, i:i + 1], res[:, t, :],
                                           ALU.mult, ALU.add).then_inc(sm["x3_made"], 1)
                statistics(LN3, b, lambda i: res[:, b * TB + i, :], "x3_made")

            def route(b):
                n = b + 1
                dve.wait_ge(sm["lg_done"], n)
                v.tensor_copy(lg[:, :, :], ps_lg).then_inc(sm["lg_copied"], 1)
                dve.wait_ge(sm["lg_copied"], n)
                v.tensor_reduce(mx[:, b, :], lg[:, :, :], AX.X, ALU.max).then_inc(sm["mx_made"], 1)
                dve.wait_ge(sm["mx_made"], n)
                v.tensor_tensor(cand[:, :, :], lg[:, :, :], mx[:, b, :].unsqueeze(2).to_broadcast([P, TB, E]), ALU.is_equal).then_inc(sm["eq_made"], 1)
                dve.wait_ge(sm["eq_made"], n)
                dve.wait_ge(consts_made, 1)
                v.tensor_tensor(cand[:, :, :], cand[:, :, :], io_e8[:, :, :], ALU.mult).then_inc(sm["cand_made"], 1)
                dve.wait_ge(sm["cand_made"], n)
                v.tensor_reduce(idx[:, :], cand[:, :, :], AX.X, ALU.min).then_inc(sm["idx_made"], 1)
                dve.wait_ge(sm["idx_made"], n)
                v.tensor_tensor(onehot[:, b * TB:(b + 1) * TB, :], io_e8[:, :, :],
                                idx[:, :].unsqueeze(2).to_broadcast([P, TB, E]), ALU.is_equal).then_inc(sm["onehot_made"], 1)

            def destination(b):
                n = b + 1
                tiles = slice(b * TB, (b + 1) * TB)
                dve.wait_ge(sm["rank_done"], n)
                if b == B - 1:
                    v.tensor_copy(cnt[:, :], ps_count[0:1, :]).then_inc(counts_made, 1)
                v.tensor_tensor(row_e[:, :, :], ps_rank, io_reg[:, :, :], ALU.add).then_inc(sm["row_made"], 1)
                dve.wait_ge(sm["row_made"], n)
                v.tensor_tensor(row_e[:, :, :], row_e[:, :, :], onehot[:, tiles, :], ALU.mult).then_inc(sm["row_picked"], 1)
                dve.wait_ge(sm["row_picked"], n)
                v.tensor_reduce(dest_f[:, tiles], row_e[:, :, :], AX.X, ALU.add).then_inc(sm["dest_summed"], 1)
                dve.wait_ge(sm["dest_summed"], n)
                v.tensor_copy(dest[:, tiles], dest_f[:, tiles]).then_inc(sm["dest_made"], 1)

            def slot_table(_):
                step = [0]

                def link(ins):
                    step[0] += 1
                    ins.then_inc(table_step, 1)
                    dve.wait_ge(table_step, step[0])

                link(v.tensor_tensor(cmp_k[:, :, :], io_k[0:1, :, :], ps_count[0:1, :].unsqueeze(2).to_broadcast([1, E, NT]), ALU.is_lt))
                link(v.tensor_reduce(ntile[:, :], cmp_k[:, :, :], AX.X, ALU.add))
                link(v.tensor_tensor_scan(incl[:, :], one_e[:, :], ntile[:, :], 0.0, ALU.mult, ALU.add))
                link(v.tensor_scalar(tile_s[:, :], io_s[:, :], incl[:, E - 1:E], None, ALU.min))
                link(v.tensor_tensor(cmp_s[:, :, :], tile_s[:, :].unsqueeze(2).to_broadcast([1, NS, E]),
                                     incl[:, :].unsqueeze(1).to_broadcast([1, NS, E]), ALU.is_ge))
                link(v.tensor_reduce(te_f[:, :], cmp_s[:, :, :], AX.X, ALU.add))
                link(v.tensor_tensor(cmp_s[:, :, :], cmp_s[:, :, :], ntile[:, :].unsqueeze(1).to_broadcast([1, NS, E]), ALU.mult))
                link(v.tensor_reduce(before[:, :], cmp_s[:, :, :], AX.X, ALU.add))
                link(v.tensor_tensor(tr_f[:, :], tile_s[:, :], before[:, :], ALU.subtract))
                link(v.tensor_scalar(tr_f[:, :], tr_f[:, :], float(P), None, ALU.mult))
                v.tensor_scalar(te[:, :], te_f[:, :], E - 1.0, None, ALU.min)
                v.scalar_tensor_tensor(tr[:, :], te_f[:, :], float(REGION), tr_f[:, :], ALU.mult, ALU.add).then_inc(table_made, 1)

            def shared_hidden(b):
                h = hs[:, b % 2]
                dve.wait_ge(sm["th_made"], b + 1)
                v.scalar_tensor_tensor(h, h, 1.0, psG, ALU.add, ALU.mult).then_inc(sm["ht_made"], 1)
                dve.wait_ge(sm["ht_made"], b + 1)
                dve.wait_ge(sm["shu_done"], b + 1)
                v.tensor_tensor(h, h, psQ, ALU.mult).then_inc(sm["h_made"], 1)

            def shared_add(b):
                rows_b = res[:, b * TB:(b + 1) * TB, :]
                dve.wait_ge(sm["sd_done"], b + 1)
                v.scalar_tensor_tensor(rows_b, psV, 0.5, rows_b, ALU.mult, ALU.add).then_inc(sm["base_made"], 1)

            def split_router():
                dve.wait_ge(small_in["rw"], 16)
                v.tensor_copy(rw_hi[:, :, :], rw[:, :, :]).then_inc(rw_split, 1)
                dve.wait_ge(rw_split, 1)
                v.tensor_tensor(rw_lo[:, :, :], rw[:, :, :], f32(rw_hi[:, :, :]), ALU.subtract).then_inc(rw_split, 1)

            steps = {"stats1": stats1, "norm1": norm1, "weight_lo": weight_lo, "turned1_lo": turned1_lo,
                     "memory": memory, "residual2": residual2, "sim_stats": sim_stats,
                     "sim_centre": sim_centre, "sim_scale": sim_scale, "residual3": residual3,
                     "turned3_lo": turned3_lo, "route": route, "destination": destination, "slot_table": slot_table,
                     "shared_hidden": shared_hidden, "shared_add": shared_add}
            for name, n in steps_of(DVE_ORDER):
                steps[name](n)
                if (name, n) == ("memory", 0):
                    split_router()

            def hidden(s, r):
                dve.wait_ge(rth_made, s + 1)
                v.scalar_tensor_tensor(rh[:, r, :], rh[:, r, :], 1.0, psGU[r][:, 0:D], ALU.add, ALU.mult).then_inc(rt_made, 1)
                dve.wait_ge(rt_made, s + 1)
                v.tensor_tensor(rh[:, r, :], rh[:, r, :], psGU[r][:, D:2 * D], ALU.mult).then_inc(rh_made, 1)

            def rows_lo(s, r, q):
                dve.wait_ge(xg_hi_made, s + 1)
                v.tensor_tensor(xgT_lo[:, r], psX[r][:, :, 0:P], f32(xgT_hi[:, r]), ALU.subtract).then_inc(xg_lo_made, 1)
                v.tensor_copy(tid[:, bass.ds(s, 1)], xg[:, q, D:D + 1].bitcast(U32)).then_inc(tid_made, 1)

            def hidden_lo(s, r):
                dve.wait_ge(hT_hi_made, s + 1)
                v.tensor_tensor(hT_lo[:, r], psH[r][:, :, 0:P], f32(hT_hi[:, r]), ALU.subtract).then_inc(hT_lo_made, 1)

            def result(s, r, n, q, m):
                dve.wait_ge(down_done, s + 1)
                dve.wait_ge(rb_in[q], (m + 1) * 16)
                dve.wait_ge(written[r], n * 16)
                v.scalar_tensor_tensor(ry[:, r, :], psY[r][:, 0, :], 0.5, rb[:, q, :], ALU.mult, ALU.add).then_inc(y_made, 1)

            rows_lo(0, 0, 0)
            rows_lo(1, 1, 1)
            hidden(0, 0)
            rows_lo(2, 0, 2)
            for s in range(PEEL):
                hidden(s + 1, (s + 1) % 2)
                hidden_lo(s, s % 2)
                if s >= 1:
                    result(s - 1, (s - 1) % 2, (s - 1) // 2, (s - 1) % TILE_RING, (s - 1) // TILE_RING)
                rows_lo(s + 3, (s + 1) % 2, (s + 3) % TILE_RING)
            with dve.Fori(0, ROUNDS) as i:
                for j in range(TILE_RING):
                    s = i * TILE_RING + (PEEL + j)
                    r = (PEEL + j) % 2
                    hidden(s + 1, 1 - r)
                    hidden_lo(s, r)
                    done = PEEL + j - 1
                    result(s - 1, 1 - r, i * (TILE_RING // 2) + done // 2, done % TILE_RING, i + done // TILE_RING)
                    rows_lo(s + 3, 1 - r, (PEEL + j + 3) % TILE_RING)
            for s in range(PEEL + ROUNDS * TILE_RING, NS + 1):
                if s + 1 < NS:
                    hidden(s + 1, (s + 1) % 2)
                if s < NS:
                    hidden_lo(s, s % 2)
                result(s - 1, (s - 1) % 2, (s - 1) // 2, (s - 1) % TILE_RING, (s - 1) // TILE_RING)
                if s + 3 < NS:
                    rows_lo(s + 3, (s + 1) % 2, (s + 3) % TILE_RING)

        @block.tensor
        def _(pe):
            T = nc.tensor

            def product(out_ap, pairs):
                terms = [(a, c) for a, _, c, _ in pairs] + [(b, c) for _, b, c, _ in pairs] + [(a, d) for a, _, _, d in pairs]
                for i, (l, r) in enumerate(terms):
                    last = T.matmul(out_ap, l, r, start=(i == 0), stop=(i == len(terms) - 1))
                return last

            def turn(ps, rows_of, done):
                for i in range(TB):
                    for k in range(KT):
                        last = T.transpose(ps[:, k, i * P:(i + 1) * P], rows_of[:, i, k * P:(k + 1) * P], ident[:, :])
                last.then_inc(sm[done], 1)

            def turn1(b):
                if b == 0:
                    pe.wait_ge(ident_made, 1)
                pe.wait_ge(sm["xn1_made"], b + 1)
                if b >= 1:
                    pe.wait_ge(sm["xT1_lo_made"], b)
                turn(psT, xn1[:, b % 2], "t1_done")

            def turn2(b):
                pe.wait_ge(sm["xn2_made"], b + 1)
                if b == 0:
                    pe.wait_ge(kvT_made[0], 1)
                else:
                    pe.wait_ge(sm["mixT_made"], b)
                turn(psU, xn2, "t2_done")

            def turn3(b):
                pe.wait_ge(sm["xn3_made"], b + 1)
                if b == 0:
                    pe.wait_ge(kvT_made[1], 1)
                else:
                    pe.wait_ge(sm["lg_copied"], b)
                turn(psM, xn3[:, b % 2], "t3_done")

            def project(b, w, ps, done, read, reads=1):
                pe.wait_ge(proj_lo, w + 1)
                pe.wait_ge(sm["xT1_hi_made"], b + 1)
                pe.wait_ge(sm["xT1_lo_made"], b + 1)
                if b >= 1:
                    pe.wait_ge(sm[read], b * reads)
                for m in range(KT):
                    last = product(ps[:, m, :], [(gqv_hi[:, w, k, m * P:(m + 1) * P], gqv_lo[:, w, k, m * P:(m + 1) * P],
                                                  xT1_hi[:, b % 2, k, :], xT1_lo[:, b % 2, k, :]) for k in range(KT)])
                last.then_inc(sm[done], 1)

            def turn_wk(_):
                pe.wait_ge(small_in["wk"], 16)
                pe.wait_ge(ident_made, 1)
                T.transpose(bM[0:C, 0:C], wk_nat[:, :], ident[0:C, 0:C]).then_inc(wk_t, 1)

            def turn_ctx(h):
                pe.wait_ge(small_in["ctx"], 16)
                pe.wait_ge(ident_made, 1)
                for t in range(NT // 2):
                    last = T.transpose((bO, bS)[h][0:C, t * P:(t + 1) * P], ctx_nat[:, h * (NT // 2) + t, :], ident[:, :])
                last.then_inc(ctx_t[h], 1)

            def kv(h):
                pe.wait_ge(ctxT_made[h], 1)
                pe.wait_ge(wkT_made, 1)
                for i in range(2):
                    last = T.matmul((psU, psM)[h][0:C, i, :], wkT[:, :], ctxT(2 * h + i), start=True, stop=True)
                last.then_inc(kv_done[h], 1)

            def turn_kv(_):
                pe.wait_ge(kvT_made[0], 1)
                pe.wait_ge(kvT_made[1], 1)
                pe.wait_ge(ctxT_made[1], 1)
                for b in range(B):
                    for k in range(KT):
                        last = T.transpose(ps_kv[:, b, k, :], kvT(b)[:, k * P:(k + 1) * P], ident[0:C, 0:C])
                last.then_inc(kv_rows_done, 1)

            def recall(b):
                pe.wait_ge(small_in["wo"], 16)
                pe.wait_ge(sm["loaded"], b + 1)
                if b == 0:
                    pe.wait_ge(ctxT_made[0], 1)
                else:
                    pe.wait_ge(sm["x2_made"], b * TB)
                for i in range(TB):
                    for m in range(KT):
                        last = T.matmul(psO[:, i, :], tq[:, b % 2, m, i * P:(i + 1) * P], wo[:, m, :],
                                        start=(m == 0), stop=(m == KT - 1))
                last.then_inc(sm["o_done"], 1)

            def context_mix(b):
                pe.wait_ge(kv_rows_made, 1)
                pe.wait_ge(sm["xT2_made"], b + 1)
                for k in range(KT):
                    last = T.matmul(bU[0:C, 0:S], kv_rows[:, b, k, :], xT2[:, b % 2, k, :], start=(k == 0), stop=(k == KT - 1))
                last.then_inc(sm["mix_done"], 1)

            def similarity(b):
                pe.wait_ge(sm["mixT_made"], b + 1)
                if b == 0:
                    pe.wait_ge(kv_rows_made, 1)
                else:
                    pe.wait_ge(sm["centred"], b)
                for i in range(TB):
                    last = T.matmul(psS[:, i, :], mixT[:, b % 2, i * P:(i + 1) * P], kvT(b), start=True, stop=True)
                last.then_inc(sm["sim_done"], 1)

            def router(b):
                pe.wait_ge(rw_split, 2)
                pe.wait_ge(sm["xT3_hi_made"], b + 1)
                pe.wait_ge(sm["xT3_lo_made"], b + 1)
                product(ps_lgT, [(rw_hi[:, k, :], rw_lo[:, k, :], xT3_hi[:, b % 2, k, :], xT3_lo[:, b % 2, k, :])
                                 for k in range(KT)]).then_inc(sm["lgT_done"], 1)

            def router_turn(b):
                pe.wait_ge(sm["lgT_copied"], b + 1)
                for i in range(TB):
                    last = T.transpose(ps_lg[:, i, :], lgT[:, i * P:(i + 1) * P], ident[0:E, 0:E])
                last.then_inc(sm["lg_done"], 1)

            def rank(b):
                pe.wait_ge(consts_made, 1)
                pe.wait_ge(dve_consts, 2)
                pe.wait_ge(sm["onehot_made"], b + 1)
                if b == 0:
                    pe.wait_ge(sm["xT1_lo_made"], B)
                else:
                    pe.wait_ge(sm["row_made"], b)
                first = b * TB
                T.matmul(ps_rank, below[:, :], onehot[:, first:first + TB, :], start=True, stop=False)
                for t in range(first):
                    T.matmul(ps_rank, ones[:, :], onehot[:, t, :].unsqueeze(1).to_broadcast([P, TB, E]), start=False, stop=False)
                for i in range(1, TB):
                    for t in range(first, first + i):
                        last = T.matmul(ps_rank[:, i, :], ones[:, :], onehot[:, t, :], start=False, stop=True)
                if b == B - 1:
                    for t in range(NT):
                        last = T.matmul(ps_count, ones[:, :], onehot[:, t, :], start=(t == 0), stop=(t == NT - 1))
                last.then_inc(sm["rank_done"], 1)

            def shared(b, w, ps, done, read):
                pe.wait_ge(unit_lo, w + 1)
                pe.wait_ge(sm["xT3_hi_made"], b + 1)
                pe.wait_ge(sm["xT3_lo_made"], b + 1)
                pe.wait_ge(sm[read], B)
                if b >= 1:
                    pe.wait_ge(sm["h_made"], b)
                for m in range(KT):
                    last = product(ps[:, m, :], [(shw_hi[:, w, k, m * P:(m + 1) * P], shw_lo[:, w, k, m * P:(m + 1) * P],
                                                  xT3_hi[:, b % 2, k, :], xT3_lo[:, b % 2, k, :]) for k in range(KT)])
                last.then_inc(sm[done], 1)

            def shared_down(b):
                pe.wait_ge(small_in["shd"], 16)
                pe.wait_ge(sm["h_made"], b + 1)
                pe.wait_ge(sm["stored"], B * KT)
                if b >= 1:
                    pe.wait_ge(sm["base_made"], b)
                for i in range(TB):
                    for k in range(KT):
                        last = T.matmul(psV[:, i, :], hs[:, b % 2, k, i * P:(i + 1) * P], shd[:, k, :],
                                        start=(k == 0), stop=(k == KT - 1))
                last.then_inc(sm["sd_done"], 1)

            steps = {"turn1": turn1, "turn2": turn2, "turn3": turn3, "turn_wk": turn_wk, "turn_ctx": turn_ctx,
                     "kv": kv, "turn_kv": turn_kv, "context_mix": context_mix, "recall": recall, "similarity": similarity,
                     "gate": lambda b: project(b, 0, psG, "g_done", "tg_made"),
                     "query": lambda b: project(b, 1, psQ, "q_done", "tq_made"),
                     "value": lambda b: project(b, 2, psV, "v_done", "stored", KT),
                     "router": router, "router_turn": router_turn, "rank": rank,
                     "shared_gate": lambda b: shared(b, 0, psG, "shg_done", "tg_made"),
                     "shared_up": lambda b: shared(b, 1, psQ, "shu_done", "tq_made"),
                     "shared_down": shared_down}
            for name, n in steps_of(PE_ORDER):
                steps[name](n)

            def rows_turn(s, r, q, loads, reused):
                pe.wait_ge(xg_in[q], loads * 16)
                if reused:
                    pe.wait_ge(xg_lo_made, s - 1)
                for k in range(KT):
                    last = T.transpose(psX[r][:, k, 0:P], xg[:, q, k * P:(k + 1) * P], ident[:, :])
                last.then_inc(tx_done, 1)

            def experts(first, n):
                _, values = nc.values_load_multi_w_load_instructions(
                    te[0:1, bass.ds(first, n)], engines=[mybir.EngineType.PE], min_val=0, max_val=E - 1,
                    skip_runtime_bounds_check_because="slot_table counts experts up from 0 and clamps to E - 1")
                return values

            def gate_up(s, r, e, reused):
                pe.wait_ge(xg_lo_made, s + 1)
                if reused:
                    pe.wait_ge(rh_made, s - 1)
                product(psGU[r][:, :], [(xgT_hi[:, r, k, :], xgT_lo[:, r, k, :], gu_hi[:, e, k, :], gu_lo[:, e, k, :])
                                        for k in range(KT)]).then_inc(gu_done, 1)

            def hidden_turn(s, r, reused):
                pe.wait_ge(rh_made, s + 1)
                if reused:
                    pe.wait_ge(hT_lo_made, s - 1)
                for k in range(KT):
                    last = T.transpose(psH[r][:, k, 0:P], rh[:, r, k * P:(k + 1) * P], ident[:, :])
                last.then_inc(th_done, 1)

            def down(s, r, e, reused):
                pe.wait_ge(hT_lo_made, s + 1)
                if reused:
                    pe.wait_ge(y_made, s - 1)
                product(psY[r][:, 0, :], [(hT_hi[:, r, k, :], hT_lo[:, r, k, :], dn_hi[:, e, k, :], dn_lo[:, e, k, :])
                                          for k in range(KT)]).then_inc(down_done, 1)

            pe.wait_ge(table_made, 1)
            pe.wait_ge(unit_lo, len(units) - PROJ)
            rows_turn(0, 0, 0, 1, False)
            rows_turn(1, 1, 1, 1, False)
            pe.wait_ge(sm["h_made"], B)
            e = experts(0, PEEL + 2)
            gate_up(0, 0, e[0], False)
            rows_turn(2, 0, 2, 1, True)
            gate_up(1, 1, e[1], False)
            pe.wait_ge(sm["base_made"], B)
            for s in range(PEEL):
                hidden_turn(s, s % 2, s >= 2)
                if s >= 1:
                    down(s - 1, (s - 1) % 2, e[s - 1], False)
                rows_turn(s + 3, (s + 1) % 2, (s + 3) % TILE_RING, (s + 3) // TILE_RING + 1, True)
                gate_up(s + 2, s % 2, e[s + 2], True)
            with pe.Fori(0, ROUNDS) as i:
                e = experts(i * TILE_RING + (PEEL - 1), TILE_RING + 3)
                for j in range(TILE_RING):
                    s = i * TILE_RING + (PEEL + j)
                    r = (PEEL + j) % 2
                    hidden_turn(s, r, True)
                    down(s - 1, 1 - r, e[j], True)
                    rows_turn(s + 3, 1 - r, (PEEL + j + 3) % TILE_RING, i + ((PEEL + j + 3) // TILE_RING + 1), True)
                    gate_up(s + 2, r, e[j + 3], True)
            assert PEEL + ROUNDS * TILE_RING == REST
            e = experts(REST - 1, NS - REST + 1)
            for s in range(REST, NS + 1):
                if s < NS:
                    hidden_turn(s, s % 2, True)
                down(s - 1, (s - 1) % 2, e[s - REST], True)
                if s + 3 < NS:
                    rows_turn(s + 3, (s + 1) % 2, (s + 3) % TILE_RING, (s + 3) // TILE_RING + 1, True)
                if s + 2 < NS:
                    gate_up(s + 2, s % 2, e[s + 3 - REST], True)


_INS = ["x", "ctx_512", "L0_attn_Wv", "L0_attn_Wg", "L0_attn_bg", "L0_attn_Wq", "L0_attn_bq", "L0_attn_Wo",
        "L0_xattn_W_k", "L0_xattn_b_k", "L0_xattn_ln_gamma", "L0_xattn_ln_beta", "L0_ffn_router_w",
        "L0_ffn_gate_w", "L0_ffn_up_w", "L0_ffn_down_w", "L0_ffn_shared_gate_w", "L0_ffn_shared_up_w",
        "L0_ffn_shared_down_w"]


def kernel(**inputs):
    import numpy as _np
    import concourse.bacc as _bacc
    from concourse import mybir as _mybir
    from concourse.bass_utils import run_bass_kernel_spmd as _run

    nc = _bacc.Bacc("TRN2", target_bir_lowering=False, num_devices=1)
    arrays, args = {}, []
    for name in _INS:
        a = _np.ascontiguousarray(inputs[name])
        arrays[f"in_{name}_dram"] = a
        args.append(nc.dram_tensor(f"in_{name}_dram", a.shape, _mybir.dt.from_np(a.dtype), kind="ExternalInput").ap())
    shape = inputs["x"].shape
    args.append(nc.dram_tensor("out_0_dram", shape, _mybir.dt.float32, kind="ExternalOutput").ap())
    decoder_kernel(nc, *args)
    r = _run(nc, [arrays], core_ids=[0])
    return r.results[0]["out_0_dram"]
```
